# Optimizing a Trainium2 kernel written in Bass

```python
import numpy as np
import jax
import jax.numpy as jnp

def _softmax(x, axis=-1):
    return jax.nn.softmax(x, axis=axis)

def _gelu(x):
    return jax.nn.gelu(x, approximate=True)

def _silu(x):
    return jax.nn.silu(x)

def _sigmoid(x):
    return jax.nn.sigmoid(x)

def _layernorm(x, axis=-1, eps=1e-05):
    m = jnp.mean(x, axis=axis, keepdims=True)
    v = jnp.var(x, axis=axis, keepdims=True)
    return (x - m) / jnp.sqrt(v + eps)

def _scatter_add(tgt, idx, src, axis=0):
    return tgt.at[idx].add(src)

def _segment_sum(src, seg, n):
    return jax.ops.segment_sum(src, seg, n)
kernel_name = 'mk_gnn_preln_d2_gnn_r8_af65fc'

def setup_inputs(seed: int=0):
    np.random.seed(seed)
    _w = jnp.asarray

    def _rec_inputs():
        import jax
        import jax.numpy as jnp
        _gk = jax.random.key(seed)
        x = -0.000202 + 1 * jax.random.normal(jax.random.fold_in(_gk, 1), (12500, 64), jnp.float32)
        _s = jax.random.randint(jax.random.fold_in(_gk, 2), (100000,), 0, 12500, jnp.int32)
        _d = jax.random.randint(jax.random.fold_in(_gk, 3), (100000,), 0, 12500, jnp.int32)
        _loop = jnp.arange(12500, dtype=jnp.int32)
        src = jnp.concatenate([_s, _d, _loop])
        dst = jnp.concatenate([_d, _s, _loop])
        _o = jnp.argsort(dst, stable=True)
        src = src[_o]
        dst = dst[_o]
        edge_attr_64 = -8.16379e-05 + 0.999858 * jax.random.normal(jax.random.fold_in(_gk, 12), (212500, 64), jnp.float32)
        return (x, src, dst, edge_attr_64)
    x, src, dst, edge_attr_64 = _rec_inputs()

    def _L0_gnn_setup():
        import jax, jax.numpy as jnp
        import numpy as np
        N_NODES = 12500
        N_EDGES = 200000
        IN_SIZE = 64
        OUT_SIZE = 64
        N_HEADS = 2
        NEG_SLOPE = 0.2
        BN_EPS = 1e-05
        key = jax.random.key(seed)
        ks = jax.random.split(key, 8)
        atom = jax.random.normal(ks[0], (N_NODES, IN_SIZE), dtype=jnp.float32)
        bond = jax.random.normal(ks[1], (N_EDGES, IN_SIZE), dtype=jnp.float32)
        W = jax.random.normal(ks[2], (IN_SIZE, OUT_SIZE * N_HEADS), dtype=jnp.float32) * 0.1
        attn_l = jax.random.normal(ks[3], (N_HEADS, OUT_SIZE), dtype=jnp.float32) * 0.1
        attn_r = jax.random.normal(ks[4], (N_HEADS, OUT_SIZE), dtype=jnp.float32) * 0.1
        bn_gamma = jnp.ones((OUT_SIZE,), dtype=jnp.float32)
        bn_beta = jnp.zeros((OUT_SIZE,), dtype=jnp.float32)
        src = jax.random.randint(ks[5], (N_EDGES,), 0, N_NODES, dtype=jnp.int32)
        dst = jax.random.randint(ks[6], (N_EDGES,), 0, N_NODES, dtype=jnp.int32)
        return {'atom': atom, 'bond': bond, 'W': W, 'attn_l': attn_l, 'attn_r': attn_r, 'bn_gamma': bn_gamma, 'bn_beta': bn_beta, 'src': src, 'dst': dst}
    _L0_gnn_all = _L0_gnn_setup()
    _L0_gnn_in = {k: v for k, v in _L0_gnn_all.items() if k in ('W', 'attn_l', 'attn_r', 'bn_gamma', 'bn_beta')}
    del _L0_gnn_all

    def _L1_gnn_setup():
        import jax, jax.numpy as jnp
        import numpy as np
        N_NODES = 6250
        N_EDGES = 100000
        D = 64
        NEG_SLOPE = 0.2

        def _gat_conv(x, src, dst, W, a_src, a_dst, b, n_nodes):
            h = x @ W
            alpha_s = h @ a_src
            alpha_d = h @ a_dst
            e = alpha_s[src] + alpha_d[dst]
            e = jnp.where(e > 0, e, NEG_SLOPE * e)
            m = jax.ops.segment_max(e, dst, num_segments=n_nodes)
            m = jnp.where(jnp.isfinite(m), m, 0.0)
            ex = jnp.exp(e - m[dst])
            s = jax.ops.segment_sum(ex, dst, num_segments=n_nodes)
            alpha = ex / (s[dst] + 1e-16)
            out = jax.ops.segment_sum(alpha[:, None] * h[src], dst, num_segments=n_nodes)
            return out + b

        def _add_self_loops(edge_index, n_nodes):
            loop = jnp.arange(n_nodes, dtype=edge_index.dtype)
            src = jnp.concatenate([edge_index[0], loop])
            dst = jnp.concatenate([edge_index[1], loop])
            return (src, dst)
        key = jax.random.key(seed)
        ks = jax.random.split(key, 16)
        x = jax.random.normal(ks[0], (N_NODES, D), dtype=jnp.float32)
        edge_index = jax.random.randint(ks[1], (2, N_EDGES), 0, N_NODES, dtype=jnp.int32)
        sc = 1.0 / np.sqrt(D)

        def lin(k):
            return jax.random.uniform(k, (D, D), jnp.float32, -sc, sc)

        def att(k):
            return jax.random.uniform(k, (D,), jnp.float32, -sc, sc)
        return {'x': x, 'edge_index': edge_index, 'W1': lin(ks[2]), 'a1s': att(ks[3]), 'a1d': att(ks[4]), 'b1': jnp.zeros((D,), jnp.float32), 'W2': lin(ks[5]), 'a2s': att(ks[6]), 'a2d': att(ks[7]), 'b2': jnp.zeros((D,), jnp.float32), 'W3': lin(ks[8]), 'a3s': att(ks[9]), 'a3d': att(ks[10]), 'b3': jnp.zeros((D,), jnp.float32)}
    _L1_gnn_all = _L1_gnn_setup()
    _L1_gnn_in = {k: v for k, v in _L1_gnn_all.items() if k in ('W1', 'a1s', 'a1d', 'b1', 'W2', 'a2s', 'a2d', 'b2', 'W3', 'a3s', 'a3d', 'b3')}
    del _L1_gnn_all
    return {'x': x, 'src': src, 'dst': dst, 'edge_attr_64': edge_attr_64, 'L0_gnn_W': _L0_gnn_in['W'], 'L0_gnn_attn_l': _L0_gnn_in['attn_l'], 'L0_gnn_attn_r': _L0_gnn_in['attn_r'], 'L0_gnn_bn_gamma': _L0_gnn_in['bn_gamma'], 'L0_gnn_bn_beta': _L0_gnn_in['bn_beta'], 'L1_gnn_W1': _L1_gnn_in['W1'], 'L1_gnn_a1s': _L1_gnn_in['a1s'], 'L1_gnn_a1d': _L1_gnn_in['a1d'], 'L1_gnn_b1': _L1_gnn_in['b1'], 'L1_gnn_W2': _L1_gnn_in['W2'], 'L1_gnn_a2s': _L1_gnn_in['a2s'], 'L1_gnn_a2d': _L1_gnn_in['a2d'], 'L1_gnn_b2': _L1_gnn_in['b2'], 'L1_gnn_W3': _L1_gnn_in['W3'], 'L1_gnn_a3s': _L1_gnn_in['a3s'], 'L1_gnn_a3d': _L1_gnn_in['a3d'], 'L1_gnn_b3': _L1_gnn_in['b3']}

def reference(x, src, dst, edge_attr_64, L0_gnn_W, L0_gnn_attn_l, L0_gnn_attn_r, L0_gnn_bn_gamma, L0_gnn_bn_beta, L1_gnn_W1, L1_gnn_a1s, L1_gnn_a1d, L1_gnn_b1, L1_gnn_W2, L1_gnn_a2s, L1_gnn_a2d, L1_gnn_b2, L1_gnn_W3, L1_gnn_a3s, L1_gnn_a3d, L1_gnn_b3):
    import jax
    import jax.numpy as jnp

    def _L0_gnn_ref(atom, bond, W, attn_l, attn_r, bn_gamma, bn_beta, src, dst):
        import jax, jax.numpy as jnp
        import numpy as np
        N_NODES = 12500
        N_EDGES = 200000
        IN_SIZE = 64
        OUT_SIZE = 64
        N_HEADS = 2
        NEG_SLOPE = 0.2
        BN_EPS = 1e-05
        N = atom.shape[0]
        H, D = attn_l.shape
        h_edge = ((atom[src] + bond) @ W).reshape(-1, H, D)
        h_node = (atom @ W).reshape(-1, H, D)
        el = jnp.einsum('ehd,hd->eh', h_edge, attn_l)
        er = jnp.einsum('nhd,hd->nh', h_node, attn_r)
        s = el + er[dst]
        s = jnp.where(s > 0, s, NEG_SLOPE * s)
        smax = jax.ops.segment_max(s, dst, num_segments=N)
        ex = jnp.exp(s - smax[dst])
        denom = jax.ops.segment_sum(ex, dst, num_segments=N)
        alpha = ex / denom[dst]
        ft = jax.ops.segment_sum(h_edge * alpha[..., None], dst, num_segments=N)
        h = ft.mean(axis=1)
        mu = h.mean(axis=0)
        var = h.var(axis=0)
        h = (h - mu) / jnp.sqrt(var + BN_EPS) * bn_gamma + bn_beta
        h = jax.nn.relu(h)
        return h

    def _L1_gnn_ref(x, edge_index, W1, a1s, a1d, b1, W2, a2s, a2d, b2, W3, a3s, a3d, b3):
        import jax, jax.numpy as jnp
        import numpy as np
        N_NODES = 6250
        N_EDGES = 100000
        D = 64
        NEG_SLOPE = 0.2

        def _gat_conv(x, src, dst, W, a_src, a_dst, b, n_nodes):
            h = x @ W
            alpha_s = h @ a_src
            alpha_d = h @ a_dst
            e = alpha_s[src] + alpha_d[dst]
            e = jnp.where(e > 0, e, NEG_SLOPE * e)
            m = jax.ops.segment_max(e, dst, num_segments=n_nodes)
            m = jnp.where(jnp.isfinite(m), m, 0.0)
            ex = jnp.exp(e - m[dst])
            s = jax.ops.segment_sum(ex, dst, num_segments=n_nodes)
            alpha = ex / (s[dst] + 1e-16)
            out = jax.ops.segment_sum(alpha[:, None] * h[src], dst, num_segments=n_nodes)
            return out + b

        def _add_self_loops(edge_index, n_nodes):
            loop = jnp.arange(n_nodes, dtype=edge_index.dtype)
            src = jnp.concatenate([edge_index[0], loop])
            dst = jnp.concatenate([edge_index[1], loop])
            return (src, dst)
        n = x.shape[0]
        src, dst = _add_self_loops(edge_index, n)
        h = _gat_conv(x, src, dst, W1, a1s, a1d, b1, n)
        h = jax.nn.relu(h)
        h = _gat_conv(h, src, dst, W2, a2s, a2d, b2, n)
        h = jax.nn.relu(h)
        return _gat_conv(h, src, dst, W3, a3s, a3d, b3, n)
    edge_index = jnp.stack([src, dst])
    h = jnp.maximum(_layernorm(x, axis=-1), 0.0)
    x = x + _L0_gnn_ref(h, edge_attr_64, L0_gnn_W, L0_gnn_attn_l, L0_gnn_attn_r, L0_gnn_bn_gamma, L0_gnn_bn_beta, src, dst)
    h = jnp.maximum(_layernorm(x, axis=-1), 0.0)
    x = x + _L1_gnn_ref(h, edge_index, L1_gnn_W1, L1_gnn_a1s, L1_gnn_a1d, L1_gnn_b1, L1_gnn_W2, L1_gnn_a2s, L1_gnn_a2d, L1_gnn_b2, L1_gnn_W3, L1_gnn_a3s, L1_gnn_a3d, L1_gnn_b3)
    return x

_drawn_inputs = setup_inputs


def setup_inputs(seed=0):
    import zlib

    import numpy as np

    out = dict(_drawn_inputs(seed))
    spreads = {'L0_gnn_bn_gamma': (1.0, 0.2),
     'L0_gnn_bn_beta': (0.0, 0.1),
     'L1_gnn_b1': (0.0, 0.8),
     'L1_gnn_b2': (0.0, 0.281),
     'L1_gnn_b3': (0.0, 0.1)}
    factors = {'L1_gnn_a1s': 8.0,
     'L1_gnn_a1d': 64.0,
     'L1_gnn_W2': 3.038,
     'L1_gnn_a2s': 63.779,
     'L1_gnn_a2d': 59.845,
     'L1_gnn_a3s': 64.0,
     'L1_gnn_a3d': 64.0}
    for name, (base, spread) in spreads.items():
        noise = np.random.default_rng([zlib.crc32(name.encode()), seed]).standard_normal(out[name].shape)
        drawn = base * np.exp(spread * noise) if base else spread * noise
        out[name] = jnp.asarray(drawn.astype(out[name].dtype))
    for name, factor in factors.items():
        out[name] = (out[name] * factor).astype(out[name].dtype)
    return out
```

```python
from contextlib import ExitStack

import concourse.bass as bass
from concourse import mybir

F32 = mybir.dt.float32
I32 = mybir.dt.int32
BF16 = mybir.dt.bfloat16
ALU = mybir.AluOpType
ACT = mybir.ActivationFunctionType
AX = mybir.AxisListType

P = 128
D = 64
NB = 125
Q = 18
CAP = P * Q
GROUP = 4
BANK = 512
CHUNKS = -(-Q // GROUP)
SLOPE = 0.2
EPS = 1e-5
BIG = float(2 ** 80)
ROW = D + 2


def bcast(ap, axis, count):
    wide = ap.unsqueeze(axis)
    shape = list(wide.shape)
    shape[axis] = count
    return wide.to_broadcast(shape)


def chunk_cols(g):
    return range(g * GROUP, min((g + 1) * GROUP, Q))


class Constants:

    def __init__(self, nc, ctx):
        def sb(name, shape, dt=F32):
            return ctx.enter_context(nc.sbuf_tensor(name, shape, dt))
        self.ident = sb("ident", [P, P])
        self.ones = sb("ones", [P, P])
        self.iota_nodes = sb("iota_nodes", [P, NB])
        self.eps = sb("eps", [P, 1])
        self.unit_count = sb("unit_count", [1, 1], I32)
        self.nc = nc
        self.taken = []

    def sem(self, name):
        self.taken.append(self.nc.alloc_semaphore(name=name))
        return self.taken[-1]

    def end_phase(self):
        self.nc.clear_and_free_semaphores(self.taken)
        self.nc.all_engine_barrier()
        self.taken = []


def wait_apart(eng, sem, value, passed):
    eng.wait_ge(sem, value)
    eng.sem_inc(passed, 1)


def own_steps(eng, chain, base=0):
    count = {}

    def step(ins, signal=None):
        signal, before = (chain, base) if signal is None else (signal, 0)
        count[id(signal)] = count.get(id(signal), 0) + 1
        ins.then_inc(signal, 1)
        eng.wait_ge(signal, before + count[id(signal)])
    step.taken = lambda: count[id(chain)]
    return step


def list_units(nc, con, dst, unit_ints, unit_floats, n_nodes, n_edges):
    blocks = n_nodes // NB
    rows = NB
    row_len = n_edges // rows
    rounds = -(-n_edges // CAP)
    per_part = unit_ints.shape[0] // P
    assert 3 * per_part <= BANK and blocks < P and rows <= P
    with ExitStack() as ctx:
        def sb(name, shape, dt=F32):
            return ctx.enter_context(nc.sbuf_tensor(name, shape, dt))

        def ps(name):
            return ctx.enter_context(nc.psum_tensor(name, [P, BANK], F32))

        dst_rows = sb("dst_rows", [rows, row_len], I32)
        dst_next = sb("dst_next", [rows, row_len], I32)
        falls = sb("falls", [rows, row_len])
        fallen = sb("fallen", [rows, 1])
        first_dst = sb("first_dst", [rows, 1])
        thr_row = sb("thr_row", [rows, blocks + 1])
        thr_col = sb("thr_col", [blocks + 1, 1])
        below = sb("below", [rows, blocks + 1])
        row_of = sb("row_of", [blocks + 1, 1])
        row_of_i = sb("row_of_i", [blocks + 1, 1], I32)
        edge_row = sb("edge_row", [blocks + 1, row_len], I32)
        edge_row_f = sb("edge_row_f", [blocks + 1, row_len])
        inner = sb("inner", [blocks + 1, 1])
        is_sorted = sb("is_sorted", [blocks + 1, 1])
        all_edges = sb("all_edges", [blocks + 1, 1])
        start = sb("start", [blocks + 1, 1])
        step_mat = sb("step_mat", [blocks + 1, blocks])
        cum_mat = sb("cum_mat", [blocks, blocks])
        size = sb("size", [blocks, 1])
        caps = sb("caps", [blocks, rounds])
        over = sb("over", [blocks, rounds])
        units_extra = sb("units_extra", [blocks, 1])
        steps = sb("steps", [blocks, 3])
        ends = sb("ends", [blocks, 1])
        unit_row = sb("unit_row", [blocks, P * per_part])
        past = sb("past", [blocks, P * per_part])
        unit_id = sb("unit_id", [P, per_part])
        sums = sb("sums", [P, per_part, 3])
        rnd = sb("rnd", [P, per_part])
        edge0 = sb("edge0", [P, per_part])
        ints = sb("ints", [P, per_part, 2], I32)
        floats = sb("floats", [P, per_part, 4])
        ps_before, ps_falls, ps_steps, ps_ends = ps("ps_before"), ps("ps_falls"), ps("ps_steps"), ps("ps_ends")
        ps_sums, ps_total = ps("ps_sums"), ps("ps_total")

        sem = con.sem
        dst_loaded, rows_gathered, stored = sem("dst_loaded"), sem("rows_gathered"), sem("list_stored")
        const_made, chain = sem("const_made"), sem("list_chain")
        below_made, falls_counted, row_known, starts_known = (
            sem("below_made"), sem("falls_counted"), sem("row_known"), sem("starts_known"))
        units_known, past_made, list_made = sem("units_known"), sem("past_made"), sem("list_made")
        before_summed, falls_summed, steps_summed, ends_summed, units_summed = (
            sem("before_summed"), sem("falls_summed"), sem("steps_summed"), sem("ends_summed"),
            sem("units_summed"))
        MADE = 13

        with nc.Block() as block:
            @block.sync
            def _(sp):
                def rows_of(off):
                    return dst[off:off + n_edges].rearrange("(p j) -> p j", p=rows)
                sp.dma_start(dst_rows[:, :], rows_of(0)).then_inc(dst_loaded, 16)
                sp.dma_start(dst_next[:, :], rows_of(1)).then_inc(dst_loaded, 16)
                sp.wait_ge(list_made, 4)
                sp.dma_start(unit_ints.rearrange("(p c) k -> p c k", p=P), ints[:, :, :]).then_inc(stored, 16)
                sp.dma_start(unit_floats.rearrange("(p c) k -> p c k", p=P), floats[:, :, :]).then_inc(stored, 16)
                sp.wait_ge(stored, 32)

            @block.gpsimd
            def _(gp):
                def iota(out, pattern, base=0, channel=0):
                    gp.iota(out, pattern, base=base, channel_multiplier=channel,
                            allow_small_or_imprecise_dtypes=True).then_inc(const_made, 1)

                def where(out, compare, fill, base, n, column=-1):
                    gp.affine_select(out=out, in_=out, compare_op=compare, fill=fill, base=base,
                                     pattern=[[column, n]], channel_multiplier=-column
                                     ).then_inc(const_made, 1)
                iota(thr_row[:, :], [[NB, blocks + 1]])
                iota(thr_col[:, :], [[0, 1]], channel=NB)
                iota(con.iota_nodes[:, :], [[1, NB]])
                iota(caps[:, :], [[CAP, rounds]], base=CAP)
                iota(unit_id[:, :], [[1, per_part]], channel=per_part)
                gp.memset(con.ident[:, :], 0.0).then_inc(const_made, 1)
                gp.memset(step_mat[:, :], 0.0).then_inc(const_made, 1)
                gp.memset(cum_mat[:, :], 1.0).then_inc(const_made, 1)
                gp.wait_ge(const_made, 8)
                where(con.ident[:, :], ALU.not_equal, 1.0, 0, P)
                where(step_mat[:, :], ALU.not_equal, 1.0, -1, blocks)
                where(cum_mat[:, :], ALU.is_ge, 0.0, 0, blocks, column=1)
                gp.wait_ge(const_made, 11)
                where(step_mat[:, :], ALU.not_equal, -1.0, 0, blocks)
                iota(unit_row[:, :], [[1, P * per_part]])
                gp.wait_ge(row_known, 1)
                gp.indirect_dma_start(edge_row[:, :], None, dst[0:n_edges].rearrange("(p j) -> p j", p=rows),
                                      bass.IndirectOffsetOnAxis(ap=row_of_i[:, 0:1], axis=0)
                                      ).then_inc(rows_gathered, 16)
                gp.wait_ge(rows_gathered, 16)

            @block.vector
            def _(ve):
                step = own_steps(ve, chain)
                step(ve.memset(con.ones[:, :], 1.0))
                step(ve.memset(con.eps[:, :], EPS))
                step(ve.memset(steps[:, 0:1], 1.0))
                ve.wait_ge(dst_loaded, 32)
                ve.wait_ge(const_made, MADE)
                step(ve.tensor_copy(first_dst[:, :], dst_rows[:, 0:1]))
                step(ve.tensor_scalar(below[:, :], thr_row[:, :], first_dst[:, 0:1], None, ALU.is_gt),
                     below_made)
                ve.wait_ge(before_summed, 1)
                step(ve.tensor_scalar(row_of[:, :], ps_before[0:blocks + 1, 0:1], -1.0, 0.0, ALU.add, ALU.max))
                step(ve.tensor_copy(row_of_i[:, :], row_of[:, :]), row_known)
                step(ve.tensor_tensor(falls[:, :], dst_rows[:, :], dst_next[:, :], ALU.is_gt))
                step(ve.tensor_reduce(fallen[:, :], falls[:, :], AX.X, ALU.add), falls_counted)
                ve.wait_ge(rows_gathered, 16)
                step(ve.tensor_copy(edge_row_f[:, :], edge_row[:, :]))
                step(ve.tensor_scalar(edge_row_f[:, :], edge_row_f[:, :], thr_col[:, 0:1], None, ALU.is_lt))
                step(ve.tensor_reduce(inner[:, :], edge_row_f[:, :], AX.X, ALU.add))
                ve.wait_ge(falls_summed, 1)
                step(ve.tensor_scalar(is_sorted[:, :], ps_falls[0:blocks + 1, 0:1], 0.0, None, ALU.is_equal))
                step(ve.scalar_tensor_tensor(start[:, :], row_of[:, :], float(row_len), inner[:, :],
                                             ALU.mult, ALU.add))
                step(ve.tensor_scalar(start[:, :], start[:, :], is_sorted[:, 0:1], None, ALU.mult), starts_known)
                step(ve.tensor_scalar(all_edges[:, :], is_sorted[:, :], float(-n_edges), float(n_edges),
                                      ALU.mult, ALU.add))
                ve.wait_ge(steps_summed, 1)
                step(ve.tensor_copy(steps[:, 2:3], ps_steps[0:blocks, 0:1]))
                step(ve.tensor_tensor(size[:, :], steps[:, 2:3], all_edges[0:blocks, :], ALU.add))
                step(ve.tensor_scalar(over[:, :], caps[:, :], size[:, 0:1], None, ALU.is_lt))
                step(ve.tensor_reduce(units_extra[:, :], over[:, :], AX.X, ALU.add))
                step(ve.tensor_scalar(steps[:, 1:2], units_extra[:, :], 1.0, None, ALU.add), units_known)
                ve.wait_ge(ends_summed, 1)
                step(ve.tensor_copy(ends[:, :], ps_ends[0:blocks, 0:1]))
                step(ve.tensor_copy(con.unit_count[:, :], ps_total[0:1, 0:1]))
                step(ve.tensor_scalar(past[:, :], unit_row[:, :], ends[:, 0:1], None, ALU.is_ge), past_made)
                ve.wait_ge(units_summed, 1)
                step(ve.tensor_copy(sums[:, :, :].rearrange("p c k -> p (c k)"), ps_sums[:, 0:3 * per_part]))
                step(ve.tensor_tensor(rnd[:, :], unit_id[:, :], sums[:, :, 1], ALU.subtract))
                step(ve.scalar_tensor_tensor(edge0[:, :], rnd[:, :], float(CAP), sums[:, :, 2],
                                             ALU.mult, ALU.add))
                step(ve.tensor_scalar(edge0[:, :], edge0[:, :], float(n_edges), None, ALU.min))
                step(ve.tensor_scalar(floats[:, :, 0], sums[:, :, 0], float(NB), None, ALU.mult))
                step(ve.tensor_scalar(floats[:, :, 1], rnd[:, :], 0.0, None, ALU.is_gt))
                step(ve.tensor_copy(ints[:, :, 0], floats[:, :, 0]), list_made)
                step(ve.tensor_copy(ints[:, :, 1], edge0[:, :]), list_made)
                step(ve.tensor_scalar(floats[:, :, 2], floats[:, :, 1], -1.0, 1.0, ALU.mult, ALU.add), list_made)
                step(ve.tensor_scalar(floats[:, :, 3], floats[:, :, 1], BIG, -BIG, ALU.mult, ALU.add), list_made)

            @block.tensor
            def _(te):
                te.wait_ge(below_made, 1)
                te.matmul(ps_before[0:blocks + 1, 0:1], below[:, :], con.ones[0:rows, 0:1]).then_inc(before_summed, 1)
                te.wait_ge(falls_counted, 1)
                te.matmul(ps_falls[:, 0:1], con.ones[0:rows, :], fallen[:, :]).then_inc(falls_summed, 1)
                te.wait_ge(starts_known, 1)
                te.matmul(ps_steps[0:blocks, 0:1], step_mat[:, :], start[:, :]).then_inc(steps_summed, 1)
                te.wait_ge(units_known, 1)
                te.matmul(ps_total[0:1, 0:1], steps[:, 1:2], con.ones[0:blocks, 0:1])
                te.matmul(ps_ends[0:blocks, 0:1], cum_mat[:, :], steps[:, 1:2]).then_inc(ends_summed, 1)
                te.wait_ge(past_made, 1)
                for c in range(per_part):
                    ins = te.matmul(ps_sums[:, 3 * c:3 * c + 3], past[0:blocks - 1, c::per_part],
                                    steps[0:blocks - 1, :])
                ins.then_inc(units_summed, 1)


def layer_norm_relu(e, step, con, x, out, square, small, nb, to_act, from_act):
    mean, var, rstd = small
    step(e.tensor_reduce(mean, x, AX.X, ALU.add))
    step(e.tensor_scalar(mean, mean, 1.0 / D, None, ALU.mult))
    step(e.tensor_tensor(out, x, bcast(mean, 2, D), ALU.subtract), to_act)
    e.wait_ge(from_act, 1)
    step(e.tensor_reduce(var, square, AX.X, ALU.add), to_act)
    e.wait_ge(from_act, 2)
    step(e.reciprocal(rstd, rstd))
    step(e.tensor_tensor(out, out, bcast(rstd, 2, D), ALU.mult), to_act)


def layer_norm_act(ac, con, out, final, square, small, to_act, from_act, seen):
    mean, var, rstd = small
    ac.wait_ge(to_act, seen + 1)
    ac.activation(square, out, ACT.Square).then_inc(from_act, 1)
    ac.wait_ge(to_act, seen + 2)
    ac.activation(rstd, var, ACT.Sqrt, bias=con.eps[0:NB, 0:1], scale=1.0 / D).then_inc(from_act, 1)
    ac.wait_ge(to_act, seen + 3)
    ac.activation(final, out, ACT.Relu).then_inc(from_act, 1)


def node_products_pe(te, con, h, ps_t, ps_o, h_t, weights, width, nb, h_ready, seen, turned, turned_copied,
                     multiplied, products_copied):
    te.wait_ge(h_ready, seen)
    groups = nb // GROUP
    for g in range(groups + 1):
        if g < groups:
            if g >= 2:
                te.wait_ge(turned_copied, g - 1)
            for j in range(GROUP):
                ins = te.transpose(ps_t[g % 2][0:D, j * P:j * P + NB], h[:, g * GROUP + j, 0:D],
                                   con.ident[0:NB, 0:NB])
            ins.then_inc(turned, 1)
        if g >= 1:
            te.wait_ge(turned_copied, g)
            if g >= 3:
                te.wait_ge(products_copied, g - 2)
            for j in range(GROUP):
                ins = te.matmul(ps_o[(g - 1) % 2][0:NB, j * width:(j + 1) * width],
                                h_t[(g - 1) % 2][:, j * P:j * P + NB], weights)
            ins.then_inc(multiplied, 1)


def node_products_copy(e, ps_t, ps_o, h_t, out, width, nb, turned, turned_copied, multiplied,
                       products_copied):
    groups = nb // GROUP
    for g in range(groups + 1):
        if g < groups:
            e.wait_ge(turned, g + 1)
            if g >= 2:
                e.wait_ge(multiplied, g - 1)
            e.activation(h_t[g % 2][:, :].rearrange("p (j n) -> p j n", n=P)[:, :, 0:NB],
                         ps_t[g % 2][0:D, :].rearrange("p (j n) -> p j n", n=P)[:, :, 0:NB],
                         ACT.Copy).then_inc(turned_copied, 1)
        if g >= 1:
            e.wait_ge(multiplied, g)
            e.activation(out[:, (g - 1) * GROUP:g * GROUP, :],
                         ps_o[(g - 1) % 2][0:NB, 0:GROUP * width].rearrange("p (j w) -> p j w", w=width),
                         ACT.Copy).then_inc(products_copied, 1)


def first_nodes(nc, con, x, attn_l, attn_r, w, table, heads, n_nodes):
    nb = n_nodes // NB
    with ExitStack() as ctx:
        def sb(name, shape, dt=F32):
            return ctx.enter_context(nc.sbuf_tensor(name, shape, dt))

        def ps(name):
            return ctx.enter_context(nc.psum_tensor(name, [P, BANK], F32))
        sem = con.sem
        xs, hs, sq = sb("n0_x", [NB, nb, D]), sb("n0_h", [NB, nb, D]), sb("n0_sq", [NB, nb, D])
        small = [sb(f"n0_small{k}", [NB, nb])[:, :] for k in range(3)]
        ws, wp = sb("n0_w", [D, heads * D]), sb("n0_wp", [D, 2, heads * D])
        wa = sb("n0_wa", [D, 2 * heads])
        rows_out = sb("n0_rows", [NB, nb, D + 2 * heads])
        h_t = [sb(f"n0_ht{k}", [D, BANK]) for k in range(2)]
        ps_t, ps_o = [ps(f"n0_pt{k}") for k in range(2)], [ps(f"n0_po{k}") for k in range(2)]
        loaded, w_loaded, chain = sem("n0_loaded"), sem("n0_w_loaded"), sem("n0_chain")
        to_act, from_act, wa_made = sem("n0_to_act"), sem("n0_from_act"), sem("n0_wa_made")
        turned, turned_copied, multiplied, products_copied, stored = (
            sem("n0_turned"), sem("n0_turned_copied"), sem("n0_multiplied"), sem("n0_products_copied"),
            sem("n0_stored"))
        groups = nb // GROUP

        with nc.Block() as block:
            @block.sync
            def _(sp):
                sp.dma_start(xs[:, :, :], x.rearrange("(p b) d -> p b d", p=NB)).then_inc(loaded, 16)
                sp.dma_start(ws[:, :], w).then_inc(w_loaded, 16)
                for k, a in enumerate((attn_l, attn_r)):
                    sp.dma_start(wp[:, k, :], a.rearrange("h d -> (h d)").partition_broadcast(D)
                                 ).then_inc(w_loaded, 16)
                sp.wait_ge(products_copied, groups)
                sp.dma_start(table.rearrange("(p b) d -> p b d", p=NB), rows_out[:, :, :]).then_inc(stored, 16)
                sp.wait_ge(stored, 16)

            @block.vector
            def _(ve):
                step = own_steps(ve, chain)
                ve.wait_ge(w_loaded, 48)
                step(ve.tensor_tensor(wp[:, :, :], wp[:, :, :], bcast(ws[:, :], 1, 2), ALU.mult))
                step(ve.tensor_reduce(wa[:, :], wp[:, :, :].rearrange("p k (h d) -> p (k h) d", h=heads), AX.X,
                                      ALU.add), wa_made)
                ve.wait_ge(loaded, 16)
                layer_norm_relu(ve, step, con, xs[:, :, :], hs[:, :, :], sq[:, :, :], small, nb, to_act, from_act)

            @block.scalar
            def _(ac):
                layer_norm_act(ac, con, hs[:, :, :], rows_out[:, :, 0:D], sq[:, :, :], small, to_act, from_act, 0)
                node_products_copy(ac, ps_t, ps_o, h_t, rows_out[:, :, D:], 2 * heads, nb, turned, turned_copied,
                                   multiplied, products_copied)

            @block.tensor
            def _(te):
                te.wait_ge(wa_made, 1)
                node_products_pe(te, con, rows_out, ps_t, ps_o, h_t, wa[:, :], 2 * heads, nb, from_act, 3, turned,
                                 turned_copied, multiplied, products_copied)


def extend_weights(nc, sb, name, w, a_src, a_dst):
    return sb(name + "_wx", [D, ROW]), sb(name + "_as", [D, D]), sb(name + "_ad", [D, D]), sb(name + "_wp", [D, D])


def load_extended(sp, ext, w, a_src, a_dst, loaded):
    wx, a_s, a_d, _ = ext
    sp.dma_start(wx[:, 0:D], w).then_inc(loaded, 16)
    sp.dma_start(a_s[:, :], a_src.partition_broadcast(D)).then_inc(loaded, 16)
    sp.dma_start(a_d[:, :], a_dst.partition_broadcast(D)).then_inc(loaded, 16)


def make_extended(ve, step, ext):
    wx, a_s, a_d, wp = ext
    for k, a in enumerate((a_s, a_d)):
        step(ve.tensor_tensor(wp[:, :], wx[:, 0:D], a[:, :], ALU.mult))
        step(ve.tensor_reduce(wx[:, D + k:D + k + 1], wp[:, :], AX.X, ALU.add))


def middle_nodes(nc, con, x, h0, gamma, beta, w, a_src, a_dst, x_mid, table, n_nodes):
    nb = n_nodes // NB
    with ExitStack() as ctx:
        def sb(name, shape, dt=F32):
            return ctx.enter_context(nc.sbuf_tensor(name, shape, dt))

        def ps(name):
            return ctx.enter_context(nc.psum_tensor(name, [P, BANK], F32))
        sem = con.sem
        xs, hs, sq = sb("n1_x", [NB, nb, D]), sb("n1_h", [NB, nb, D]), sb("n1_sq", [NB, nb, D])
        small = [sb(f"n1_small{k}", [NB, nb])[:, :] for k in range(3)]
        rows_out = sb("n1_rows", [NB, nb, ROW])
        gm, bt = sb("n1_gamma", [NB, D]), sb("n1_beta", [NB, D])
        part, stat, root = sb("n1_part", [NB, D]), sb("n1_stat", [NB, D]), sb("n1_root", [NB, D])
        ext = extend_weights(nc, sb, "n1", w, a_src, a_dst)
        h_t = [sb(f"n1_ht{k}", [D, BANK]) for k in range(2)]
        ps_t, ps_o = [ps(f"n1_pt{k}") for k in range(2)], [ps(f"n1_po{k}") for k in range(2)]
        ps_stat = ps("n1_stat_ps")
        loaded, w_loaded, chain, w_made = sem("n1_loaded"), sem("n1_w_loaded"), sem("n1_chain"), sem("n1_w_made")
        to_act, from_act = sem("n1_to_act"), sem("n1_from_act")
        centred, squared, var_known, rooted = sem("n1_centred"), sem("n1_squared"), sem("n1_var"), sem("n1_rooted")
        part_made, summed, mid_made = sem("n1_part_made"), sem("n1_summed"), sem("n1_mid_made")
        turned, turned_copied, multiplied, products_copied, stored = (
            sem("n1_turned"), sem("n1_turned_copied"), sem("n1_multiplied"), sem("n1_products_copied"),
            sem("n1_stored"))
        groups = nb // GROUP

        def by_feature(t):
            return t[:, :, :].rearrange("p b d -> p d b")

        with nc.Block() as block:
            @block.sync
            def _(sp):
                sp.dma_start(hs[:, :, :], h0.rearrange("(p b) d -> p b d", p=NB)).then_inc(loaded, 16)
                sp.dma_start(xs[:, :, :], x.rearrange("(p b) d -> p b d", p=NB)).then_inc(loaded, 16)
                sp.dma_start(gm[:, :], gamma.partition_broadcast(NB)).then_inc(loaded, 16)
                sp.dma_start(bt[:, :], beta.partition_broadcast(NB)).then_inc(loaded, 16)
                load_extended(sp, ext, w, a_src, a_dst, w_loaded)
                sp.wait_ge(mid_made, 1)
                sp.dma_start(x_mid.rearrange("(p b) d -> p b d", p=NB), xs[:, :, :]).then_inc(stored, 16)
                sp.wait_ge(products_copied, groups)
                sp.dma_start(table.rearrange("(p b) d -> p b d", p=NB), rows_out[:, :, :]).then_inc(stored, 16)
                sp.wait_ge(stored, 32)

            @block.vector
            def _(ve):
                step = own_steps(ve, chain)
                ve.wait_ge(w_loaded, 48)
                make_extended(ve, own_steps(ve, w_made), ext)
                ve.wait_ge(loaded, 64)
                step(ve.tensor_reduce(part[:, :], by_feature(hs), AX.X, ALU.add), part_made)
                ve.wait_ge(summed, 1)
                step(ve.tensor_scalar(stat[:, :], ps_stat[0:NB, 0:D], 1.0 / n_nodes, None, ALU.mult))
                step(ve.tensor_tensor(hs[:, :, :], hs[:, :, :], bcast(stat[:, :], 1, nb), ALU.subtract), centred)
                ve.wait_ge(squared, 1)
                step(ve.tensor_reduce(part[:, :], by_feature(sq), AX.X, ALU.add), part_made)
                ve.wait_ge(rooted, 1)
                step(ve.reciprocal(root[:, :], root[:, :]))
                step(ve.tensor_tensor(root[:, :], root[:, :], gm[:, :], ALU.mult))
                step(ve.tensor_tensor(hs[:, :, :], hs[:, :, :], bcast(root[:, :], 1, nb), ALU.mult))
                step(ve.tensor_tensor(hs[:, :, :], hs[:, :, :], bcast(bt[:, :], 1, nb), ALU.add))
                step(ve.scalar_tensor_tensor(xs[:, :, :], hs[:, :, :], 0.0, xs[:, :, :], ALU.max, ALU.add), mid_made)
                layer_norm_relu(ve, step, con, xs[:, :, :], hs[:, :, :], sq[:, :, :], small, nb, to_act, from_act)

            @block.scalar
            def _(ac):
                ac.wait_ge(centred, 1)
                ac.activation(sq[:, :, :], hs[:, :, :], ACT.Square).then_inc(squared, 1)
                ac.wait_ge(summed, 2)
                ac.activation(root[:, :], ps_stat[0:NB, 0:D], ACT.Sqrt, bias=con.eps[0:NB, 0:1],
                              scale=1.0 / n_nodes).then_inc(rooted, 1)
                layer_norm_act(ac, con, hs[:, :, :], hs[:, :, :], sq[:, :, :], small, to_act, from_act, 0)
                node_products_copy(ac, ps_t, ps_o, h_t, rows_out, ROW, nb, turned, turned_copied,
                                   multiplied, products_copied)

            @block.tensor
            def _(te):
                for k in range(2):
                    te.wait_ge(part_made, k + 1)
                    te.matmul(ps_stat[0:NB, 0:D], con.ones[0:NB, 0:NB], part[:, :]).then_inc(summed, 1)
                te.wait_ge(w_made, 4)
                node_products_pe(te, con, hs, ps_t, ps_o, h_t, ext[0][:, :], ROW, nb, from_act, 3, turned,
                                 turned_copied, multiplied, products_copied)


def attention_layer(nc, con, name, units, src, dst, table, out, edge_attr=None, attn_l=None, w_out=None,
                    bias=None, residual=None, next_weights=None):
    unit_ints, unit_floats = units
    first = edge_attr is not None
    heads = 2 if first else 1
    row = D + 2 * heads
    part = D + 1
    vals = 2 * heads
    out_cols = D if (first or residual is not None) else ROW
    PARTS = 3
    SCORE_AT = BANK // 2
    PROJ_AT = P
    MAX_AT = BANK // 2
    with ExitStack() as ctx:
        def sb(tag, shape, dt=F32):
            return ctx.enter_context(nc.sbuf_tensor(f"{name}_{tag}", shape, dt))

        def ps(tag):
            return ctx.enter_context(nc.psum_tensor(f"{name}_{tag}", [P, BANK], F32))

        def sem(tag):
            return con.sem(f"{name}_{tag}")

        def two(make, tag, *args):
            return [make(f"{tag}{k}", *args) for k in range(2)]

        unit_int = two(sb, "unit_int", [1, 2], I32)
        unit_par = two(sb, "unit_par", [P, 4])
        idx = two(sb, "idx", [P, Q], I32)
        dst_ids = two(sb, "dst_ids", [P, Q], I32)
        rows_in = two(sb, "rows_in", [P, Q, row])
        own = two(sb, "own", [NB, row])
        out_sb = two(sb, "out_sb", [NB, out_cols])
        dst_local = sb("dst_local", [P, Q])
        onehot = two(sb, "onehot", [P, Q, NB])
        onehot_t = sb("onehot_t", [NB, CAP], BF16)
        mask = sb("mask", [P, Q, NB], BF16)
        masked = sb("masked", [P, heads, Q, NB])
        column_max = sb("column_max", [P, heads, NB])
        max_src = sb("max_src", [NB, heads])
        max_unit = sb("max_unit", [NB, heads])
        max_before = sb("max_before", [NB, heads])
        max_state = sb("max_state", [NB, heads])
        rescale = sb("rescale", [NB, heads])
        node_vals = sb("node_vals", [NB, vals])
        rest = sb("rest", [NB, vals])
        node_split = sb("node_split", [NB, PARTS, vals], BF16)
        edge_vals = sb("edge_vals", [P, Q, vals])
        logits = sb("logits", [P, Q, heads])
        weights = sb("weights", [P, Q, heads])
        weighted = sb("weighted", [P, Q, heads * part])
        acc = sb("acc", [NB, heads * part])
        inverse = sb("inverse", [NB, heads])
        result = sb("result", [NB, heads * D])
        result_t = sb("result_t", [heads * D, NB])
        if first:
            edges = two(sb, "edges", [P, Q, D])
            pairs_t = sb("pairs_t", [P, Q // 2, P])
            edge_scores = sb("edge_scores", [P, Q, heads])
            scores_sum = sb("scores_sum", [P, Q, heads])
            w_cols = sb("w_cols", [P, heads * D])
            al = sb("al", [P, heads * D])
            wl = sb("wl", [P, heads])
            pair_w = sb("pair_w", [P, 2 * heads])
            w_heads = sb("w_heads", [P, D])
        else:
            bias_sb = sb("bias_sb", [NB, D])
            self_row = sb("self_row", [NB, part])
            self_max = sb("self_max", [NB, 1])
            if residual is not None:
                res_sb = sb("res_sb", [NB, D])
            else:
                ext = extend_weights(nc, sb, "ext", *next_weights)

        ps_big = [ps(f"ps_big{g}") for g in range(CHUNKS)]
        ps_edge, ps_acc, ps_out = ps("ps_edge"), ps("ps_acc"), ps("ps_out")

        int_loaded, idx_loaded, meta_loaded, own_loaded, gathered, stored, edges_loaded = (
            two(sem, tag) for tag in ("int_loaded", "idx_loaded", "meta_loaded", "own_loaded",
                                      "gathered", "stored", "edges_loaded"))
        rows_taken = two(sem, "rows_taken")
        res_loaded, w_loaded, w_made, state_set = (
            sem("res_loaded"), sem("w_loaded"), sem("w_made"), sem("state_set"))
        chain = sem("chain")
        passed_sp, passed_gp, passed_te = sem("passed_sp"), sem("passed_gp"), sem("passed_te")
        local_made, onehot_built, turned, onehot_copied, mask_made = (
            sem("local_made"), sem("onehot_built"), sem("turned"), sem("onehot_copied"), sem("mask_made"))
        pairs_turned, pairs_copied, scored, scores_copied, scores_ready = (
            sem("pairs_turned"), sem("pairs_copied"), sem("scored"), sem("scores_copied"), sem("scores_ready"))
        masked_made, columns_maxed, maxima_turned = (
            sem("masked_made"), sem("columns_maxed"), sem("maxima_turned"))
        split_made, expanded, logits_made, weights_made = (
            sem("split_made"), sem("expanded"), sem("logits_made"), sem("weights_made"))
        rows_weighted, aggregated = sem("rows_weighted"), sem("aggregated")
        result_made, result_turned, result_copied, projected, out_made = (
            sem("result_made"), sem("result_turned"), sem("result_copied"), sem("projected"), sem("out_made"))

        def unit_pairs(eng):
            count = eng.value_load(con.unit_count[0:1, 0:1], min_val=1, max_val=unit_ints.shape[0] - 2)
            return eng.snap((count + 1) // 2)

        with nc.Block() as block:
            @block.sync
            def _(sp):
                pairs = unit_pairs(sp)

                def node0_of(h):
                    return sp.value_load(unit_int[h][0:1, 0:1], min_val=0, max_val=table.shape[0] - NB)

                def window(array, edge0):
                    return array[bass.ds(edge0, CAP)].rearrange("(p t) -> p t", p=P)

                def wait_used(sem, value, wait):
                    if wait:
                        wait_apart(sp, sem, value, passed_sp)

                def load_unit(u, h, k, wait):
                    sp.dma_start(unit_int[h][:, :], unit_ints[bass.ds(u, 1), :]).then_inc(int_loaded[h], 16)
                    wait_apart(sp, int_loaded[h], 16 * k + 16, passed_sp)
                    node0 = node0_of(h)
                    edge0 = sp.value_load(unit_int[h][0:1, 1:2], min_val=0, max_val=src.shape[0] - CAP)
                    wait_used(gathered[h], 16 * Q * k, wait)
                    sp.dma_start(idx[h][:, :], window(src, edge0)).then_inc(idx_loaded[h], 16)
                    wait_used(onehot_built, 2 * k + h - 1, wait)
                    sp.dma_start(dst_ids[h][:, :], window(dst, edge0)).then_inc(meta_loaded[h], 16)
                    wait_used(expanded, 2 * k + h - 1, wait)
                    sp.dma_start(unit_par[h][:, :], unit_floats[bass.ds(u, 1), :].to_broadcast([P, 4])
                                 ).then_inc(meta_loaded[h], 16)
                    sp.dma_start(own[h][:, :], table[bass.ds(node0, NB), :]).then_inc(own_loaded[h], 16)
                    if first:
                        wait_used(rows_weighted, 2 * k + h - 1, wait)
                        sp.dma_start(edges[h][:, :, :], edge_attr[bass.ds(edge0, CAP), :]
                                     .rearrange("(p t) d -> p t d", p=P)).then_inc(edges_loaded[h], 16)

                if first:
                    for half in range(2):
                        sp.dma_start(w_cols[half * D:(half + 1) * D, :], w_out).then_inc(w_loaded, 16)
                        sp.dma_start(w_heads[half * D:(half + 1) * D, :], w_out[:, half * D:(half + 1) * D]
                                     ).then_inc(w_loaded, 16)
                    sp.dma_start(al[:, :], attn_l.rearrange("h d -> (h d)").partition_broadcast(P)
                                 ).then_inc(w_loaded, 16)
                else:
                    sp.dma_start(bias_sb[:, :], bias.partition_broadcast(NB)).then_inc(w_loaded, 16)
                    if next_weights:
                        load_extended(sp, ext, *next_weights, w_loaded)
                for sem, count in ((stored[0], 16), (stored[1], 32), (res_loaded, 16)):
                    sp.sem_inc(sem, count)
                load_unit(0, 0, 0, False)
                load_unit(1, 1, 0, False)
                with sp.Fori(0, pairs) as i:
                    for h in range(2):
                        n = 2 * i + h
                        node0 = node0_of(h)
                        if residual is not None:
                            wait_used(out_made, n + 1, True)
                            sp.dma_start(res_sb[:, :], residual[bass.ds(node0, NB), :]).then_inc(res_loaded, 16)
                        load_unit(n + 2, h, i + 1, True)
                        wait_used(stored[1 - h], 16 * i + 32, True)
                        wait_apart(sp, out_made, n + 2, passed_sp)
                        sp.dma_start(out[bass.ds(node0, NB), :], out_sb[h][:, :]).then_inc(stored[h], 16)
                for h in range(2):
                    wait_apart(sp, idx_loaded[h], 16 * pairs + 16, passed_sp)
                    wait_apart(sp, meta_loaded[h], 32 * pairs + 32, passed_sp)
                    wait_apart(sp, own_loaded[h], 16 * pairs + 16, passed_sp)
                    if first:
                        wait_apart(sp, edges_loaded[h], 16 * pairs + 16, passed_sp)
                    wait_apart(sp, stored[h], 16 * pairs + 16 + 16 * h, passed_sp)

            @block.gpsimd
            def _(gp):
                pairs = unit_pairs(gp)
                with gp.Fori(0, pairs) as i:
                    for h in range(2):
                        gp.wait_ge(rows_taken[h], i + 1)
                        wait_apart(gp, idx_loaded[h], 16 * i + 16, passed_gp)
                        for t in range(Q):
                            gp.indirect_dma_start(rows_in[h][:, t, :], None, table[:, :],
                                                  bass.IndirectOffsetOnAxis(ap=idx[h][:, t:t + 1], axis=0)
                                                  ).then_inc(gathered[h], 16)

            @block.vector
            def _(ve):
                pairs = unit_pairs(ve)
                STEPS = 20 if first else 23

                ve.wait_ge(w_loaded, 5 * 16 if first else 4 * 16 if next_weights else 16)
                if first:
                    step = own_steps(ve, w_made)
                    step(ve.tensor_tensor(al[:, :], al[:, :], w_cols[:, :], ALU.mult))
                    step(ve.tensor_reduce(wl[:, :], al[:, :].rearrange("p (h d) -> p h d", h=heads), AX.X,
                                          ALU.add))
                    step(ve.memset(pair_w[:, :], 0.0))
                    step(ve.tensor_copy(pair_w[0:D, 0:heads], wl[0:D, :]))
                    step(ve.tensor_copy(pair_w[D:P, heads:2 * heads], wl[D:P, :]))
                elif next_weights:
                    make_extended(ve, own_steps(ve, w_made), ext)
                step = own_steps(ve, state_set)
                step(ve.memset(acc[:, :], 0.0))
                step(ve.memset(rescale[:, :], 0.0))
                step(ve.memset(max_state[:, :], 0.0))
                step(ve.memset(ps_acc[0:NB, 0:heads * part], 0.0))
                if residual is not None:
                    step(ve.memset(res_sb[:, :], 0.0))

                def build_onehot(n, k, h):
                    ve.wait_ge(meta_loaded[h], 32 * k + 32)
                    ve.tensor_scalar(dst_local[:, :], dst_ids[h][:, :], unit_par[h][:, 0:1], None,
                                     ALU.subtract).then_inc(local_made, 1)
                    ve.wait_ge(local_made, n + 1)
                    ve.tensor_tensor(onehot[h][:, :, :], bcast(con.iota_nodes[:, :], 1, Q),
                                     bcast(dst_local[:, :], 2, NB), ALU.is_equal).then_inc(onehot_built, 1)

                def finish(i, h, n, step):
                    ve.wait_ge(aggregated, n + 1)
                    ve.wait_ge(weights_made, 2 * n + 2)
                    for hd in range(heads):
                        span = slice(hd * part, (hd + 1) * part)
                        step(ve.scalar_tensor_tensor(acc[:, span], acc[:, span], rescale[:, hd:hd + 1],
                                                     ps_acc[0:NB, span], ALU.mult, ALU.add))
                    step(ve.tensor_scalar(inverse[:, :], acc[:, D::part], 1e-16, None, ALU.add))
                    step(ve.reciprocal(inverse[:, :], inverse[:, :]))
                    if first:
                        step(ve.tensor_scalar(result[:, 0:D], acc[:, 0:D], inverse[:, 0:1], None, ALU.mult))
                        ve.tensor_scalar(result[:, D:2 * D], acc[:, part:part + D], inverse[:, 1:2], None,
                                         ALU.mult).then_inc(result_made, 1)
                        return
                    ve.scalar_tensor_tensor(result[:, :], acc[:, 0:D], inverse[:, 0:1], bias_sb[:, :],
                                            ALU.mult, ALU.add).then_inc(result_made, 1)
                    if residual is not None:
                        ve.wait_ge(result_made, n + 1)
                        ve.wait_ge(res_loaded, 16 * n + 16)
                        ve.wait_ge(stored[1 - h], 16 * i + 16)
                        ve.tensor_tensor(out_sb[1 - h][:, :], result[:, :], res_sb[:, :], ALU.add
                                         ).then_inc(out_made, 1)

                def begin(h, step):
                    carries, begins, low = (unit_par[h][0:NB, k:k + 1] for k in (1, 2, 3))
                    step(ve.tensor_copy(node_vals[:, 0:heads], own[h][:, D + heads:row]))
                    if first:
                        step(ve.tensor_scalar(max_before[:, :], max_state[:, :], carries, low, ALU.mult, ALU.add))
                        return
                    step(ve.tensor_tensor(self_max[:, :], own[h][:, D:D + 1], own[h][:, D + 1:D + 2], ALU.add))
                    step(ve.scalar_tensor_tensor(self_max[:, :], self_max[:, :], SLOPE, self_max[:, :],
                                                 ALU.mult, ALU.max))
                    step(ve.tensor_scalar(self_max[:, :], self_max[:, :], begins, None, ALU.mult))
                    step(ve.scalar_tensor_tensor(max_before[:, :], max_state[:, :], carries, self_max[:, :],
                                                 ALU.mult, ALU.add))
                    ve.tensor_scalar(self_row[:, 0:D], own[h][:, 0:D], begins, None, ALU.mult)
                    step(ve.tensor_copy(self_row[:, D:part], begins))
                    step(ve.scalar_tensor_tensor(acc[:, :], acc[:, :], carries, self_row[:, :],
                                                 ALU.mult, ALU.add))

                def weigh(i, h, n, k_next, step):
                    ve.wait_ge(gathered[h], 16 * Q * i + 16 * Q)
                    ve.wait_ge(own_loaded[h], 16 * i + 16)
                    if first:
                        ve.wait_ge(scores_copied, n + 1)
                        ve.wait_ge(edges_loaded[h], 16 * i + 16)
                        ve.tensor_tensor(scores_sum[:, :, :], edge_scores[:, :, :], rows_in[h][:, :, D:D + heads],
                                         ALU.add).then_inc(scores_ready, 1)
                        ve.tensor_tensor(edges[h][:, :, :], edges[h][:, :, :], rows_in[h][:, :, 0:D], ALU.add
                                         ).then_inc(rows_taken[h], 1)
                    finish(i, h, n, step)
                    begin(h, step)
                    for hd in range(heads):
                        ve.wait_ge(masked_made, heads * n + hd + 1)
                        ve.tensor_reduce(column_max[:, hd, :], masked[:, hd, :, :].rearrange("p t n -> p n t"),
                                         AX.X, ALU.max).then_inc(columns_maxed, 1)
                    ve.wait_ge(maxima_turned, n + 1)
                    step(ve.tensor_reduce(max_src[:, :], ps_acc[0:NB, MAX_AT:MAX_AT + heads * P]
                                          .rearrange("p (h e) -> p h e", h=heads), AX.X, ALU.max))
                    step(ve.tensor_tensor(max_unit[:, :], node_vals[:, 0:heads], max_src[:, :], ALU.add))
                    step(ve.scalar_tensor_tensor(max_unit[:, :], max_unit[:, :], SLOPE, max_unit[:, :],
                                                 ALU.mult, ALU.max))
                    step(ve.tensor_tensor(node_vals[:, heads:vals], max_before[:, :], max_unit[:, :], ALU.max))
                    step(ve.tensor_copy(node_split[:, 0, :], node_vals[:, :]))
                    step(ve.tensor_tensor(rest[:, :], node_vals[:, :], node_split[:, 0, :], ALU.subtract))
                    step(ve.tensor_copy(node_split[:, 1, :], rest[:, :]))
                    ve.tensor_tensor(node_split[:, 2, :], rest[:, :], node_split[:, 1, :], ALU.subtract
                                     ).then_inc(split_made, 1)
                    step(ve.tensor_tensor(rescale[:, :], max_before[:, :], node_vals[:, heads:vals],
                                          ALU.subtract))
                    step(ve.tensor_copy(max_state[:, :], node_vals[:, heads:vals]))
                    build_onehot(n + 1, k_next, 1 - h)
                    ve.wait_ge(expanded, n + 1)
                    step(ve.tensor_reduce(edge_vals[:, :, :], ps_edge[:, 0:Q * PARTS * vals]
                                          .rearrange("p (t s k) -> p t k s", s=PARTS, k=vals), AX.X, ALU.add))
                    scores = scores_sum[:, :, :] if first else rows_in[h][:, :, D:D + 1]
                    step(ve.tensor_tensor(logits[:, :, :], scores, edge_vals[:, :, 0:heads], ALU.add))
                    step(ve.scalar_tensor_tensor(logits[:, :, :], logits[:, :, :], SLOPE, logits[:, :, :],
                                                 ALU.mult, ALU.max))
                    step(ve.tensor_tensor(logits[:, :, :], logits[:, :, :], edge_vals[:, :, heads:vals],
                                          ALU.subtract))
                    ve.tensor_scalar(logits[:, :, :], logits[:, :, :], 0.0, None, ALU.min).then_inc(logits_made, 1)
                    ve.wait_ge(weights_made, 2 * n + 4)
                    rows = edges[h] if first else rows_in[h]
                    for hd in range(heads):
                        ins = ve.tensor_tensor(weighted[:, :, hd * part:hd * part + D], rows[:, :, 0:D],
                                               bcast(weights[:, :, hd], 2, D), ALU.mult)
                    if not first:
                        ins.then_inc(rows_taken[h], 1)
                    ve.tensor_copy(weighted[:, :, D::part], weights[:, :, :]).then_inc(rows_weighted, 1)

                for h in range(2):
                    ve.sem_inc(rows_taken[h], 1)
                build_onehot(0, 0, 0)
                with ve.Fori(0, pairs) as i:
                    for h in range(2):
                        n = ve.snap(2 * i + h)
                        step = own_steps(ve, chain, ve.snap(n * STEPS))
                        weigh(i, h, n, i + h, step)
                        assert step.taken() == STEPS, step.taken()
                n = ve.snap(2 * pairs)
                finish(pairs, 0, n, own_steps(ve, chain, ve.snap(n * STEPS)))

            @block.scalar
            def _(ac):
                pairs = unit_pairs(ac)

                def prepare(n, h):
                    if first:
                        ac.wait_ge(pairs_turned, n + 1)
                        for j0 in range(0, Q // 2, GROUP):
                            j1 = min(j0 + GROUP, Q // 2)
                            ins = ac.activation(
                                pairs_t[:, j0:j1, :],
                                ps_big[j0 // GROUP][:, 0:(j1 - j0) * P].rearrange("p (j e) -> p j e", e=P),
                                ACT.Copy)
                        ins.then_inc(pairs_copied, 1)
                    ac.wait_ge(onehot_built, n + 1)
                    ac.activation(mask[:, :, :], onehot[h][:, :, :], ACT.Copy, bias=-BIG, scale=BIG
                                  ).then_inc(mask_made, 1)
                    if first:
                        ac.wait_ge(scored, n + 1)
                        ac.activation(edge_scores[:, :, :], ps_edge[:, SCORE_AT:SCORE_AT + Q * heads]
                                      .rearrange("p (t k) -> p t k", k=heads), ACT.Copy
                                      ).then_inc(scores_copied, 1)
                    ac.wait_ge(turned, n + 1)
                    for g in range(CHUNKS):
                        cols = len(chunk_cols(g)) * P
                        ins = ac.activation(onehot_t[:, g * BANK:g * BANK + cols], ps_big[g][0:NB, 0:cols],
                                            ACT.Copy)
                    ins.then_inc(onehot_copied, 1)

                def finish(i, h, n):
                    if residual is not None:
                        return
                    ac.wait_ge(result_turned, n + 1)
                    ac.activation(result_t[:, :], ps_out[0:heads * D, 0:NB], ACT.Copy if first else ACT.Relu
                                  ).then_inc(result_copied, 1)
                    ac.wait_ge(projected, n + 1)
                    ac.wait_ge(stored[1 - h], 16 * i + 16)
                    ac.activation(out_sb[1 - h][:, :], ps_out[0:NB, PROJ_AT:PROJ_AT + out_cols], ACT.Copy,
                                  scale=1.0 / heads).then_inc(out_made, 1)

                ac.sem_inc(weights_made, 2)
                prepare(0, 0)
                with ac.Fori(0, pairs) as i:
                    for h in range(2):
                        n = ac.snap(2 * i + h)
                        ac.wait_ge(mask_made, n + 1)
                        if first:
                            ac.wait_ge(scores_ready, n + 1)
                        else:
                            ac.wait_ge(gathered[h], 16 * Q * i + 16 * Q)
                        for hd in range(heads):
                            for t in range(Q):
                                score = scores_sum[:, t, hd:hd + 1] if first else rows_in[h][:, t, D:D + 1]
                                ins = ac.activation(masked[:, hd, t, :], mask[:, t, :], ACT.Identity, bias=score)
                            ins.then_inc(masked_made, 1)
                        finish(i, h, n)
                        ac.wait_ge(logits_made, n + 1)
                        ac.activation(weights[:, :, :], logits[:, :, :], ACT.Exp).then_inc(weights_made, 1)
                        ac.activation(rescale[:, :], rescale[:, :], ACT.Exp).then_inc(weights_made, 1)
                        prepare(n + 1, 1 - h)
                finish(pairs, 0, ac.snap(2 * pairs))

            @block.tensor
            def _(te):
                pairs = unit_pairs(te)

                def prepare(n, k, h):
                    if first:
                        te.wait_ge(edges_loaded[h], 16 * k + 16)
                        for j in range(Q // 2):
                            ins = te.transpose(ps_big[j // GROUP][:, j % GROUP * P:(j % GROUP + 1) * P],
                                               edges[h][:, 2 * j:2 * j + 2, :].rearrange("p t d -> p (t d)"),
                                               con.ident[:, :])
                        ins.then_inc(pairs_turned, 1)
                        te.wait_ge(pairs_copied, n + 1)
                        for j in range(Q // 2):
                            at = SCORE_AT + 2 * heads * j
                            ins = te.matmul(ps_edge[:, at:at + 2 * heads], pairs_t[:, j, :], pair_w[:, :])
                        ins.then_inc(scored, 1)
                    te.wait_ge(onehot_built, n + 1)
                    for t in range(Q):
                        ins = te.transpose(ps_big[t // GROUP][0:NB, t % GROUP * P:(t % GROUP + 1) * P],
                                           onehot[h][:, t, :], con.ident[:, :])
                    ins.then_inc(turned, 1)

                def finish(n):
                    if residual is not None:
                        return
                    wait_apart(te, result_made, n + 1, passed_te)
                    te.transpose(ps_out[0:heads * D, 0:NB], result[:, :], con.ident[0:NB, 0:NB]
                                 ).then_inc(result_turned, 1)
                    te.wait_ge(result_copied, n + 1)
                    te.matmul(ps_out[0:NB, PROJ_AT:PROJ_AT + out_cols], result_t[:, :],
                              w_heads[:, :] if first else ext[0][:, :]).then_inc(projected, 1)

                if first:
                    te.wait_ge(w_made, 5)
                elif next_weights:
                    te.wait_ge(w_made, 4)
                te.sem_inc(aggregated, 1)
                prepare(0, 0, 0)
                with te.Fori(0, pairs) as i:
                    for h in range(2):
                        n = te.snap(2 * i + h)
                        finish(n)
                        te.wait_ge(columns_maxed, heads * n + heads)
                        for hd in range(heads):
                            ins = te.transpose(ps_acc[0:NB, MAX_AT + hd * P:MAX_AT + (hd + 1) * P],
                                               column_max[:, hd, :], con.ident[:, :])
                        ins.then_inc(maxima_turned, 1)
                        te.wait_ge(onehot_copied, n + 1)
                        te.wait_ge(split_made, n + 1)
                        for t in range(Q):
                            ins = te.matmul(ps_edge[:, PARTS * vals * t:PARTS * vals * (t + 1)],
                                            onehot_t[:, t * P:(t + 1) * P],
                                            node_split[:, :, :].rearrange("p s k -> p (s k)"))
                        ins.then_inc(expanded, 1)
                        te.wait_ge(rows_weighted, n + 1)
                        for t in range(Q):
                            ins = te.matmul(ps_acc[0:NB, 0:heads * part], onehot[h][:, t, :], weighted[:, t, :],
                                            start=t == 0, stop=t == Q - 1)
                        ins.then_inc(aggregated, 1)
                        prepare(n + 1, i + h, 1 - h)
                finish(te.snap(2 * pairs))


def graph_network(nc, n_nodes, n_edges, x, src, dst, edge_attr, w0, attn_l, attn_r, gamma, beta, w1, a1s,
                  a1d, b1, w2, a2s, a2d, b2, w3, a3s, a3d, b3, out):
    blocks = n_nodes // NB
    rounds = -(-n_edges // CAP)
    grid = -(-(blocks * rounds + 2) // P) * P

    def dram(name, shape, dt=F32):
        return nc.dram_tensor(name, shape, dt).ap()
    unit_ints, unit_floats = dram("unit_ints", (grid, 2), I32), dram("unit_floats", (grid, 4))
    h_in = dram("h_in", (n_nodes, D + 4))
    h_heads, x_mid = dram("h_heads", (n_nodes, D)), dram("x_mid", (n_nodes, D))
    tables = [dram(f"table{k}", (n_nodes, ROW)) for k in range(3)]
    units = unit_ints, unit_floats
    with ExitStack() as ctx:
        con = Constants(nc, ctx)
        list_units(nc, con, dst, unit_ints, unit_floats, n_nodes, n_edges)
        con.end_phase()
        first_nodes(nc, con, x, attn_l, attn_r, w0, h_in, 2, n_nodes)
        con.end_phase()
        attention_layer(nc, con, "heads", units, src, dst, h_in, h_heads,
                        edge_attr=edge_attr, attn_l=attn_l, w_out=w0)
        con.end_phase()
        middle_nodes(nc, con, x, h_heads, gamma, beta, w1, a1s, a1d, x_mid, tables[0], n_nodes)
        plain = [(b1, (w2, a2s, a2d)), (b2, (w3, a3s, a3d)), (b3, None)]
        for k, (bias, following) in enumerate(plain):
            con.end_phase()
            attention_layer(nc, con, f"plain{k}", units, src, dst, tables[k],
                            tables[k + 1] if following else out, bias=bias, next_weights=following,
                            residual=None if following else x_mid)


NAMES = ["x", "src", "dst", "edge_attr_64", "L0_gnn_W", "L0_gnn_attn_l", "L0_gnn_attn_r", "L0_gnn_bn_gamma",
         "L0_gnn_bn_beta", "L1_gnn_W1", "L1_gnn_a1s", "L1_gnn_a1d", "L1_gnn_b1", "L1_gnn_W2", "L1_gnn_a2s",
         "L1_gnn_a2d", "L1_gnn_b2", "L1_gnn_W3", "L1_gnn_a3s", "L1_gnn_a3d", "L1_gnn_b3"]


def kernel(**inputs):
    import numpy as np
    import concourse.bacc as bacc
    from concourse.bass_utils import run_bass_kernel_spmd

    arrays = {name: np.ascontiguousarray(inputs[name]) for name in NAMES}
    n_nodes, n_edges = arrays["x"].shape[0], arrays["src"].shape[0]
    for name, fill in (("src", 0), ("dst", 2 * n_nodes), ("edge_attr_64", 0)):
        a = arrays[name]
        arrays[name] = np.concatenate([a, np.full((CAP,) + a.shape[1:], fill, a.dtype)])
    nc = bacc.Bacc("TRN2", target_bir_lowering=False, num_devices=1)
    args = [nc.dram_tensor("in_" + name, arrays[name].shape, mybir.dt.from_np(arrays[name].dtype),
                           kind="ExternalInput").ap() for name in NAMES]
    out = nc.dram_tensor("out", (n_nodes, D), F32, kind="ExternalOutput").ap()
    graph_network(nc, n_nodes, n_edges, *args, out)
    r = run_bass_kernel_spmd(nc, [{"in_" + name: arrays[name] for name in NAMES}], core_ids=[0])
    return r.results[0]["out"]
```

```python
from contextlib import ExitStack

import concourse.bass as bass
from concourse import mybir

F32 = mybir.dt.float32
I32 = mybir.dt.int32
BF16 = mybir.dt.bfloat16
ALU = mybir.AluOpType
ACT = mybir.ActivationFunctionType
AX = mybir.AxisListType

P = 128
D = 64
NB = 125
Q = 18
CAP = P * Q
TAIL_AT = P * (Q - 1)
GROUP = 4
BANK = 512
CHUNKS = -(-Q // GROUP)
SLOPE = 0.2
EPS = 1e-5
BIG = float(2 ** 80)
ROW = D + 2


def bcast(ap, axis, count):
    wide = ap.unsqueeze(axis)
    shape = list(wide.shape)
    shape[axis] = count
    return wide.to_broadcast(shape)


def chunk_cols(g):
    return range(g * GROUP, min((g + 1) * GROUP, Q))


class Constants:

    def __init__(self, nc, ctx):
        def sb(name, shape, dt=F32):
            return ctx.enter_context(nc.sbuf_tensor(name, shape, dt))
        self.ident = sb("ident", [P, P])
        self.ones = sb("ones", [P, P])
        self.iota_nodes = sb("iota_nodes", [P, NB])
        self.eps = sb("eps", [P, 1])
        self.last_unit = sb("last_unit", [1, 1], I32)
        self.nc = nc
        self.taken = []

    def sem(self, name):
        self.taken.append(self.nc.alloc_semaphore(name=name))
        return self.taken[-1]

    def end_phase(self):
        self.nc.clear_and_free_semaphores(self.taken)
        self.nc.all_engine_barrier()
        self.taken = []


def wait_apart(eng, sem, value, passed):
    eng.wait_ge(sem, value)
    eng.sem_inc(passed, 1)


def own_steps(eng, chain, base=0):
    count = {}

    def step(ins, signal=None):
        signal, before = (chain, base) if signal is None else (signal, 0)
        count[id(signal)] = count.get(id(signal), 0) + 1
        ins.then_inc(signal, 1)
        eng.wait_ge(signal, before + count[id(signal)])
    step.taken = lambda: count[id(chain)]
    return step


def list_units(nc, con, dst, unit_ints, unit_floats, n_nodes, n_edges):
    blocks = n_nodes // NB
    rows = NB
    row_len = n_edges // rows
    rounds = -(-n_edges // CAP)
    per_part = unit_ints.shape[0] // P
    assert 3 * (per_part + 1) <= BANK and blocks < P and rows <= P
    with ExitStack() as ctx:
        def sb(name, shape, dt=F32):
            return ctx.enter_context(nc.sbuf_tensor(name, shape, dt))

        def ps(name):
            return ctx.enter_context(nc.psum_tensor(name, [P, BANK], F32))

        dst_rows = sb("dst_rows", [rows, row_len], I32)
        dst_next = sb("dst_next", [rows, row_len], I32)
        falls = sb("falls", [rows, row_len])
        fallen = sb("fallen", [rows, 1])
        first_dst = sb("first_dst", [rows, 1])
        thr_row = sb("thr_row", [rows, blocks + 1])
        thr_col = sb("thr_col", [blocks + 1, 1])
        below = sb("below", [rows, blocks + 1])
        row_of = sb("row_of", [blocks + 1, 1])
        row_of_i = sb("row_of_i", [blocks + 1, 1], I32)
        edge_row = sb("edge_row", [blocks + 1, row_len], I32)
        edge_row_f = sb("edge_row_f", [blocks + 1, row_len])
        inner = sb("inner", [blocks + 1, 1])
        is_sorted = sb("is_sorted", [blocks + 1, 1])
        all_edges = sb("all_edges", [blocks + 1, 1])
        start = sb("start", [blocks + 1, 1])
        step_mat = sb("step_mat", [blocks + 1, blocks])
        cum_mat = sb("cum_mat", [blocks, blocks])
        size = sb("size", [blocks, 1])
        caps = sb("caps", [blocks, rounds])
        over = sb("over", [blocks, rounds])
        units_extra = sb("units_extra", [blocks, 1])
        steps = sb("steps", [blocks, 3])
        ends = sb("ends", [blocks, 1])
        unit_row = sb("unit_row", [blocks, (P + 1) * per_part])
        past = sb("past", [blocks, (P + 1) * per_part])
        unit_id = sb("unit_id", [P, per_part + 1])
        sums = sb("sums", [P, per_part + 1, 3])
        rnd = sb("rnd", [P, per_part + 1])
        edge0 = sb("edge0", [P, per_part + 1])
        always = sb("always", [P, 1])
        tail = sb("tail", [P, per_part])
        tails = [sb(f"tails{k}", [P, per_part]) for k in range(2)]
        earlier = sb("earlier", [P, P])
        ints = sb("ints", [P, per_part, 4], I32)
        floats = sb("floats", [P, per_part, 4])
        ps_before, ps_falls, ps_steps, ps_ends = ps("ps_before"), ps("ps_falls"), ps("ps_steps"), ps("ps_ends")
        ps_sums, ps_total = ps("ps_sums"), ps("ps_total")

        sem = con.sem
        dst_loaded, rows_gathered, stored = sem("dst_loaded"), sem("rows_gathered"), sem("list_stored")
        const_made, chain = sem("const_made"), sem("list_chain")
        below_made, falls_counted, row_known, starts_known = (
            sem("below_made"), sem("falls_counted"), sem("row_known"), sem("starts_known"))
        tails_counted, tails_summed = sem("tails_counted"), sem("tails_summed")
        units_known, past_made, list_made = sem("units_known"), sem("past_made"), sem("list_made")
        before_summed, falls_summed, steps_summed, ends_summed, units_summed = (
            sem("before_summed"), sem("falls_summed"), sem("steps_summed"), sem("ends_summed"),
            sem("units_summed"))
        MADE = 15

        with nc.Block() as block:
            @block.sync
            def _(sp):
                def rows_of(off):
                    return dst[off:off + n_edges].rearrange("(p j) -> p j", p=rows)
                sp.dma_start(dst_rows[:, :], rows_of(0)).then_inc(dst_loaded, 16)
                sp.dma_start(dst_next[:, :], rows_of(1)).then_inc(dst_loaded, 16)
                sp.wait_ge(list_made, 6)
                sp.dma_start(unit_ints.rearrange("(p c) k -> p c k", p=P), ints[:, :, :]).then_inc(stored, 16)
                sp.dma_start(unit_floats.rearrange("(p c) k -> p c k", p=P), floats[:, :, :]).then_inc(stored, 16)
                sp.wait_ge(stored, 32)

            @block.gpsimd
            def _(gp):
                def iota(out, pattern, base=0, channel=0):
                    gp.iota(out, pattern, base=base, channel_multiplier=channel,
                            allow_small_or_imprecise_dtypes=True).then_inc(const_made, 1)

                def where(out, compare, fill, base, n, column=-1):
                    gp.affine_select(out=out, in_=out, compare_op=compare, fill=fill, base=base,
                                     pattern=[[column, n]], channel_multiplier=-column
                                     ).then_inc(const_made, 1)
                iota(thr_row[:, :], [[NB, blocks + 1]])
                iota(thr_col[:, :], [[0, 1]], channel=NB)
                iota(con.iota_nodes[:, :], [[1, NB]])
                iota(caps[:, :], [[CAP, rounds]], base=CAP)
                iota(unit_id[:, :], [[1, per_part + 1]], channel=per_part)
                gp.memset(con.ident[:, :], 0.0).then_inc(const_made, 1)
                gp.memset(step_mat[:, :], 0.0).then_inc(const_made, 1)
                gp.memset(cum_mat[:, :], 1.0).then_inc(const_made, 1)
                gp.memset(earlier[:, :], 1.0).then_inc(const_made, 1)
                gp.wait_ge(const_made, 9)
                where(con.ident[:, :], ALU.not_equal, 1.0, 0, P)
                where(step_mat[:, :], ALU.not_equal, 1.0, -1, blocks)
                where(cum_mat[:, :], ALU.is_ge, 0.0, 0, blocks, column=1)
                where(earlier[:, :], ALU.is_gt, 0.0, 0, P, column=1)
                gp.wait_ge(const_made, 13)
                where(step_mat[:, :], ALU.not_equal, -1.0, 0, blocks)
                iota(unit_row[:, :], [[1, (P + 1) * per_part]])
                gp.wait_ge(row_known, 1)
                gp.indirect_dma_start(edge_row[:, :], None, dst[0:n_edges].rearrange("(p j) -> p j", p=rows),
                                      bass.IndirectOffsetOnAxis(ap=row_of_i[:, 0:1], axis=0)
                                      ).then_inc(rows_gathered, 16)
                gp.wait_ge(rows_gathered, 16)

            @block.vector
            def _(ve):
                step = own_steps(ve, chain)
                step(ve.memset(con.ones[:, :], 1.0))
                step(ve.memset(con.eps[:, :], EPS))
                step(ve.memset(steps[:, 0:1], 1.0))
                ve.wait_ge(dst_loaded, 32)
                ve.wait_ge(const_made, MADE)
                step(ve.tensor_copy(first_dst[:, :], dst_rows[:, 0:1]))
                step(ve.tensor_scalar(below[:, :], thr_row[:, :], first_dst[:, 0:1], None, ALU.is_gt),
                     below_made)
                ve.wait_ge(before_summed, 1)
                step(ve.tensor_scalar(row_of[:, :], ps_before[0:blocks + 1, 0:1], -1.0, 0.0, ALU.add, ALU.max))
                step(ve.tensor_copy(row_of_i[:, :], row_of[:, :]), row_known)
                step(ve.tensor_tensor(falls[:, :], dst_rows[:, :], dst_next[:, :], ALU.is_gt))
                step(ve.tensor_reduce(fallen[:, :], falls[:, :], AX.X, ALU.add), falls_counted)
                ve.wait_ge(rows_gathered, 16)
                step(ve.tensor_copy(edge_row_f[:, :], edge_row[:, :]))
                step(ve.tensor_scalar(edge_row_f[:, :], edge_row_f[:, :], thr_col[:, 0:1], None, ALU.is_lt))
                step(ve.tensor_reduce(inner[:, :], edge_row_f[:, :], AX.X, ALU.add))
                ve.wait_ge(falls_summed, 1)
                step(ve.tensor_scalar(always[:, :], ps_falls[:, 0:1], 0.0, None, ALU.is_gt))
                step(ve.tensor_scalar(is_sorted[:, :], ps_falls[0:blocks + 1, 0:1], 0.0, None, ALU.is_equal))
                step(ve.scalar_tensor_tensor(start[:, :], row_of[:, :], float(row_len), inner[:, :],
                                             ALU.mult, ALU.add))
                step(ve.tensor_scalar(start[:, :], start[:, :], is_sorted[:, 0:1], None, ALU.mult), starts_known)
                step(ve.tensor_scalar(all_edges[:, :], is_sorted[:, :], float(-n_edges), float(n_edges),
                                      ALU.mult, ALU.add))
                ve.wait_ge(steps_summed, 1)
                step(ve.tensor_copy(steps[:, 2:3], ps_steps[0:blocks, 0:1]))
                step(ve.tensor_tensor(size[:, :], steps[:, 2:3], all_edges[0:blocks, :], ALU.add))
                step(ve.tensor_scalar(over[:, :], caps[:, :], size[:, 0:1], None, ALU.is_lt))
                step(ve.tensor_reduce(units_extra[:, :], over[:, :], AX.X, ALU.add))
                step(ve.tensor_scalar(steps[:, 1:2], units_extra[:, :], 1.0, None, ALU.add), units_known)
                ve.wait_ge(ends_summed, 1)
                step(ve.tensor_copy(ends[:, :], ps_ends[0:blocks, 0:1]))
                step(ve.tensor_scalar(con.last_unit[:, :], ps_total[0:1, 0:1], -1.0, None, ALU.add))
                step(ve.tensor_scalar(past[:, :], unit_row[:, :], ends[:, 0:1], None, ALU.is_ge), past_made)
                ve.wait_ge(units_summed, 1)
                step(ve.tensor_copy(sums[:, :, :].rearrange("p c k -> p (c k)"), ps_sums[:, 0:3 * (per_part + 1)]))
                step(ve.tensor_tensor(rnd[:, :], unit_id[:, :], sums[:, :, 1], ALU.subtract))
                step(ve.scalar_tensor_tensor(edge0[:, :], rnd[:, :], float(CAP), sums[:, :, 2],
                                             ALU.mult, ALU.add))
                step(ve.tensor_scalar(edge0[:, :], edge0[:, :], float(n_edges), None, ALU.min))
                step(ve.tensor_scalar(floats[:, :, 0], sums[:, 0:per_part, 0], float(NB), None, ALU.mult))
                step(ve.tensor_scalar(floats[:, :, 1], rnd[:, 0:per_part], 0.0, None, ALU.is_gt))
                step(ve.tensor_tensor(tail[:, :], edge0[:, 1:per_part + 1], edge0[:, 0:per_part], ALU.subtract))
                step(ve.tensor_scalar(tail[:, :], tail[:, :], float(TAIL_AT), always[:, 0:1], ALU.is_gt, ALU.max))
                step(ve.tensor_copy(tails[0][:, :], tail[:, :]))
                now, reach = 0, 1
                while reach < per_part:
                    step(ve.tensor_copy(tails[1 - now][:, 0:reach], tails[now][:, 0:reach]))
                    step(ve.tensor_tensor(tails[1 - now][:, reach:], tails[now][:, reach:],
                                          tails[now][:, 0:per_part - reach], ALU.add))
                    now, reach = 1 - now, 2 * reach
                step(ve.tensor_copy(always[:, :], tails[now][:, per_part - 1:per_part]), tails_counted)
                ve.wait_ge(tails_summed, 1)
                step(ve.tensor_scalar(always[:, :], ps_before[:, 0:1], 0.0, None, ALU.add))
                step(ve.tensor_scalar(tails[now][:, :], tails[now][:, :], always[:, 0:1], 1.0, ALU.add, ALU.max))
                step(ve.tensor_copy(ints[:, :, 0], floats[:, :, 0]), list_made)
                step(ve.tensor_copy(ints[:, :, 1], edge0[:, 0:per_part]), list_made)
                step(ve.tensor_copy(ints[:, :, 2], tail[:, :]), list_made)
                step(ve.tensor_copy(ints[:, :, 3], tails[now][:, :]), list_made)
                step(ve.tensor_scalar(floats[:, :, 2], floats[:, :, 1], -1.0, 1.0, ALU.mult, ALU.add), list_made)
                step(ve.tensor_scalar(floats[:, :, 3], floats[:, :, 1], BIG, -BIG, ALU.mult, ALU.add), list_made)

            @block.tensor
            def _(te):
                te.wait_ge(below_made, 1)
                te.matmul(ps_before[0:blocks + 1, 0:1], below[:, :], con.ones[0:rows, 0:1]).then_inc(before_summed, 1)
                te.wait_ge(falls_counted, 1)
                te.matmul(ps_falls[:, 0:1], con.ones[0:rows, :], fallen[:, :]).then_inc(falls_summed, 1)
                te.wait_ge(starts_known, 1)
                te.matmul(ps_steps[0:blocks, 0:1], step_mat[:, :], start[:, :]).then_inc(steps_summed, 1)
                te.wait_ge(units_known, 1)
                te.matmul(ps_total[0:1, 0:1], steps[:, 1:2], con.ones[0:blocks, 0:1])
                te.matmul(ps_ends[0:blocks, 0:1], cum_mat[:, :], steps[:, 1:2]).then_inc(ends_summed, 1)
                te.wait_ge(past_made, 1)
                for c in range(per_part + 1):
                    ins = te.matmul(ps_sums[:, 3 * c:3 * c + 3], past[0:blocks - 1, c:c + (P - 1) * per_part + 1:per_part],
                                    steps[0:blocks - 1, :])
                ins.then_inc(units_summed, 1)
                te.wait_ge(tails_counted, 1)
                te.matmul(ps_before[:, 0:1], earlier[:, :], always[:, :]).then_inc(tails_summed, 1)


def layer_norm_relu(e, step, con, x, out, square, small, nb, to_act, from_act):
    mean, var, rstd = small
    step(e.tensor_reduce(mean, x, AX.X, ALU.add))
    step(e.tensor_scalar(mean, mean, 1.0 / D, None, ALU.mult))
    step(e.tensor_tensor(out, x, bcast(mean, 2, D), ALU.subtract), to_act)
    e.wait_ge(from_act, 1)
    step(e.tensor_reduce(var, square, AX.X, ALU.add), to_act)
    e.wait_ge(from_act, 2)
    step(e.reciprocal(rstd, rstd))
    step(e.tensor_tensor(out, out, bcast(rstd, 2, D), ALU.mult), to_act)


def layer_norm_act(ac, con, out, final, square, small, to_act, from_act, seen):
    mean, var, rstd = small
    ac.wait_ge(to_act, seen + 1)
    ac.activation(square, out, ACT.Square).then_inc(from_act, 1)
    ac.wait_ge(to_act, seen + 2)
    ac.activation(rstd, var, ACT.Sqrt, bias=con.eps[0:NB, 0:1], scale=1.0 / D).then_inc(from_act, 1)
    ac.wait_ge(to_act, seen + 3)
    ac.activation(final, out, ACT.Relu).then_inc(from_act, 1)


def node_products_pe(te, con, h, ps_t, ps_o, h_t, weights, width, nb, h_ready, seen, turned, turned_copied,
                     multiplied, products_copied):
    te.wait_ge(h_ready, seen)
    groups = nb // GROUP
    for g in range(groups + 1):
        if g < groups:
            if g >= 2:
                te.wait_ge(turned_copied, g - 1)
            for j in range(GROUP):
                ins = te.transpose(ps_t[g % 2][0:D, j * P:j * P + NB], h[:, g * GROUP + j, 0:D],
                                   con.ident[0:NB, 0:NB])
            ins.then_inc(turned, 1)
        if g >= 1:
            te.wait_ge(turned_copied, g)
            if g >= 3:
                te.wait_ge(products_copied, g - 2)
            for j in range(GROUP):
                ins = te.matmul(ps_o[(g - 1) % 2][0:NB, j * width:(j + 1) * width],
                                h_t[(g - 1) % 2][:, j * P:j * P + NB], weights)
            ins.then_inc(multiplied, 1)


def node_products_copy(e, ps_t, ps_o, h_t, out, width, nb, turned, turned_copied, multiplied,
                       products_copied):
    groups = nb // GROUP
    for g in range(groups + 1):
        if g < groups:
            e.wait_ge(turned, g + 1)
            if g >= 2:
                e.wait_ge(multiplied, g - 1)
            e.activation(h_t[g % 2][:, :].rearrange("p (j n) -> p j n", n=P)[:, :, 0:NB],
                         ps_t[g % 2][0:D, :].rearrange("p (j n) -> p j n", n=P)[:, :, 0:NB],
                         ACT.Copy).then_inc(turned_copied, 1)
        if g >= 1:
            e.wait_ge(multiplied, g)
            e.activation(out[:, (g - 1) * GROUP:g * GROUP, :],
                         ps_o[(g - 1) % 2][0:NB, 0:GROUP * width].rearrange("p (j w) -> p j w", w=width),
                         ACT.Copy).then_inc(products_copied, 1)


def first_nodes(nc, con, x, attn_l, attn_r, w, table, heads, n_nodes):
    nb = n_nodes // NB
    with ExitStack() as ctx:
        def sb(name, shape, dt=F32):
            return ctx.enter_context(nc.sbuf_tensor(name, shape, dt))

        def ps(name):
            return ctx.enter_context(nc.psum_tensor(name, [P, BANK], F32))
        sem = con.sem
        xs, hs, sq = sb("n0_x", [NB, nb, D]), sb("n0_h", [NB, nb, D]), sb("n0_sq", [NB, nb, D])
        small = [sb(f"n0_small{k}", [NB, nb])[:, :] for k in range(3)]
        ws, wp = sb("n0_w", [D, heads * D]), sb("n0_wp", [D, 2, heads * D])
        wa = sb("n0_wa", [D, 2 * heads])
        rows_out = sb("n0_rows", [NB, nb, D + 2 * heads])
        h_t = [sb(f"n0_ht{k}", [D, BANK]) for k in range(2)]
        ps_t, ps_o = [ps(f"n0_pt{k}") for k in range(2)], [ps(f"n0_po{k}") for k in range(2)]
        loaded, w_loaded, chain = sem("n0_loaded"), sem("n0_w_loaded"), sem("n0_chain")
        to_act, from_act, wa_made = sem("n0_to_act"), sem("n0_from_act"), sem("n0_wa_made")
        turned, turned_copied, multiplied, products_copied, stored = (
            sem("n0_turned"), sem("n0_turned_copied"), sem("n0_multiplied"), sem("n0_products_copied"),
            sem("n0_stored"))
        groups = nb // GROUP

        with nc.Block() as block:
            @block.sync
            def _(sp):
                sp.dma_start(xs[:, :, :], x.rearrange("(p b) d -> p b d", p=NB)).then_inc(loaded, 16)
                sp.dma_start(ws[:, :], w).then_inc(w_loaded, 16)
                for k, a in enumerate((attn_l, attn_r)):
                    sp.dma_start(wp[:, k, :], a.rearrange("h d -> (h d)").partition_broadcast(D)
                                 ).then_inc(w_loaded, 16)
                sp.wait_ge(products_copied, groups)
                sp.dma_start(table.rearrange("(p b) d -> p b d", p=NB), rows_out[:, :, :]).then_inc(stored, 16)
                sp.wait_ge(stored, 16)

            @block.vector
            def _(ve):
                step = own_steps(ve, chain)
                ve.wait_ge(w_loaded, 48)
                step(ve.tensor_tensor(wp[:, :, :], wp[:, :, :], bcast(ws[:, :], 1, 2), ALU.mult))
                step(ve.tensor_reduce(wa[:, :], wp[:, :, :].rearrange("p k (h d) -> p (k h) d", h=heads), AX.X,
                                      ALU.add), wa_made)
                ve.wait_ge(loaded, 16)
                layer_norm_relu(ve, step, con, xs[:, :, :], hs[:, :, :], sq[:, :, :], small, nb, to_act, from_act)

            @block.scalar
            def _(ac):
                layer_norm_act(ac, con, hs[:, :, :], rows_out[:, :, 0:D], sq[:, :, :], small, to_act, from_act, 0)
                node_products_copy(ac, ps_t, ps_o, h_t, rows_out[:, :, D:], 2 * heads, nb, turned, turned_copied,
                                   multiplied, products_copied)

            @block.tensor
            def _(te):
                te.wait_ge(wa_made, 1)
                node_products_pe(te, con, rows_out, ps_t, ps_o, h_t, wa[:, :], 2 * heads, nb, from_act, 3, turned,
                                 turned_copied, multiplied, products_copied)


def extend_weights(nc, sb, name, w, a_src, a_dst):
    return sb(name + "_wx", [D, ROW]), sb(name + "_as", [D, D]), sb(name + "_ad", [D, D]), sb(name + "_wp", [D, D])


def load_extended(sp, ext, w, a_src, a_dst, loaded):
    wx, a_s, a_d, _ = ext
    sp.dma_start(wx[:, 0:D], w).then_inc(loaded, 16)
    sp.dma_start(a_s[:, :], a_src.partition_broadcast(D)).then_inc(loaded, 16)
    sp.dma_start(a_d[:, :], a_dst.partition_broadcast(D)).then_inc(loaded, 16)


def make_extended(ve, step, ext):
    wx, a_s, a_d, wp = ext
    for k, a in enumerate((a_s, a_d)):
        step(ve.tensor_tensor(wp[:, :], wx[:, 0:D], a[:, :], ALU.mult))
        step(ve.tensor_reduce(wx[:, D + k:D + k + 1], wp[:, :], AX.X, ALU.add))


def middle_nodes(nc, con, x, h0, gamma, beta, w, a_src, a_dst, x_mid, table, n_nodes):
    nb = n_nodes // NB
    with ExitStack() as ctx:
        def sb(name, shape, dt=F32):
            return ctx.enter_context(nc.sbuf_tensor(name, shape, dt))

        def ps(name):
            return ctx.enter_context(nc.psum_tensor(name, [P, BANK], F32))
        sem = con.sem
        xs, hs, sq = sb("n1_x", [NB, nb, D]), sb("n1_h", [NB, nb, D]), sb("n1_sq", [NB, nb, D])
        small = [sb(f"n1_small{k}", [NB, nb])[:, :] for k in range(3)]
        rows_out = sb("n1_rows", [NB, nb, ROW])
        gm, bt = sb("n1_gamma", [NB, D]), sb("n1_beta", [NB, D])
        part, stat, root = sb("n1_part", [NB, D]), sb("n1_stat", [NB, D]), sb("n1_root", [NB, D])
        ext = extend_weights(nc, sb, "n1", w, a_src, a_dst)
        h_t = [sb(f"n1_ht{k}", [D, BANK]) for k in range(2)]
        ps_t, ps_o = [ps(f"n1_pt{k}") for k in range(2)], [ps(f"n1_po{k}") for k in range(2)]
        ps_stat = ps("n1_stat_ps")
        loaded, w_loaded, chain, w_made = sem("n1_loaded"), sem("n1_w_loaded"), sem("n1_chain"), sem("n1_w_made")
        to_act, from_act = sem("n1_to_act"), sem("n1_from_act")
        centred, squared, var_known, rooted = sem("n1_centred"), sem("n1_squared"), sem("n1_var"), sem("n1_rooted")
        part_made, summed, mid_made = sem("n1_part_made"), sem("n1_summed"), sem("n1_mid_made")
        turned, turned_copied, multiplied, products_copied, stored = (
            sem("n1_turned"), sem("n1_turned_copied"), sem("n1_multiplied"), sem("n1_products_copied"),
            sem("n1_stored"))
        groups = nb // GROUP

        def by_feature(t):
            return t[:, :, :].rearrange("p b d -> p d b")

        with nc.Block() as block:
            @block.sync
            def _(sp):
                sp.dma_start(hs[:, :, :], h0.rearrange("(p b) d -> p b d", p=NB)).then_inc(loaded, 16)
                sp.dma_start(xs[:, :, :], x.rearrange("(p b) d -> p b d", p=NB)).then_inc(loaded, 16)
                sp.dma_start(gm[:, :], gamma.partition_broadcast(NB)).then_inc(loaded, 16)
                sp.dma_start(bt[:, :], beta.partition_broadcast(NB)).then_inc(loaded, 16)
                load_extended(sp, ext, w, a_src, a_dst, w_loaded)
                sp.wait_ge(mid_made, 1)
                sp.dma_start(x_mid.rearrange("(p b) d -> p b d", p=NB), xs[:, :, :]).then_inc(stored, 16)
                sp.wait_ge(products_copied, groups)
                sp.dma_start(table.rearrange("(p b) d -> p b d", p=NB), rows_out[:, :, :]).then_inc(stored, 16)
                sp.wait_ge(stored, 32)

            @block.vector
            def _(ve):
                step = own_steps(ve, chain)
                ve.wait_ge(w_loaded, 48)
                make_extended(ve, own_steps(ve, w_made), ext)
                ve.wait_ge(loaded, 64)
                step(ve.tensor_reduce(part[:, :], by_feature(hs), AX.X, ALU.add), part_made)
                ve.wait_ge(summed, 1)
                step(ve.tensor_scalar(stat[:, :], ps_stat[0:NB, 0:D], 1.0 / n_nodes, None, ALU.mult))
                step(ve.tensor_tensor(hs[:, :, :], hs[:, :, :], bcast(stat[:, :], 1, nb), ALU.subtract), centred)
                ve.wait_ge(squared, 1)
                step(ve.tensor_reduce(part[:, :], by_feature(sq), AX.X, ALU.add), part_made)
                ve.wait_ge(rooted, 1)
                step(ve.reciprocal(root[:, :], root[:, :]))
                step(ve.tensor_tensor(root[:, :], root[:, :], gm[:, :], ALU.mult))
                step(ve.tensor_tensor(hs[:, :, :], hs[:, :, :], bcast(root[:, :], 1, nb), ALU.mult))
                step(ve.tensor_tensor(hs[:, :, :], hs[:, :, :], bcast(bt[:, :], 1, nb), ALU.add))
                step(ve.scalar_tensor_tensor(xs[:, :, :], hs[:, :, :], 0.0, xs[:, :, :], ALU.max, ALU.add), mid_made)
                layer_norm_relu(ve, step, con, xs[:, :, :], hs[:, :, :], sq[:, :, :], small, nb, to_act, from_act)

            @block.scalar
            def _(ac):
                ac.wait_ge(centred, 1)
                ac.activation(sq[:, :, :], hs[:, :, :], ACT.Square).then_inc(squared, 1)
                ac.wait_ge(summed, 2)
                ac.activation(root[:, :], ps_stat[0:NB, 0:D], ACT.Sqrt, bias=con.eps[0:NB, 0:1],
                              scale=1.0 / n_nodes).then_inc(rooted, 1)
                layer_norm_act(ac, con, hs[:, :, :], hs[:, :, :], sq[:, :, :], small, to_act, from_act, 0)
                node_products_copy(ac, ps_t, ps_o, h_t, rows_out, ROW, nb, turned, turned_copied,
                                   multiplied, products_copied)

            @block.tensor
            def _(te):
                for k in range(2):
                    te.wait_ge(part_made, k + 1)
                    te.matmul(ps_stat[0:NB, 0:D], con.ones[0:NB, 0:NB], part[:, :]).then_inc(summed, 1)
                te.wait_ge(w_made, 4)
                node_products_pe(te, con, hs, ps_t, ps_o, h_t, ext[0][:, :], ROW, nb, from_act, 3, turned,
                                 turned_copied, multiplied, products_copied)


def attention_layer(nc, con, name, units, src, dst, table, out, edge_attr=None, attn_l=None, w_out=None,
                    bias=None, residual=None, next_weights=None):
    unit_ints, unit_floats = units
    first = edge_attr is not None
    heads = 2 if first else 1
    row = D + 2 * heads
    part = D + 1
    vals = 2 * heads
    out_cols = D if (first or residual is not None) else ROW
    OUT_LAG = 3 if residual is None else 2
    PARTS = 3
    SCORE_AT = BANK // 2
    PROJ_AT = P
    MAX_AT = BANK // 2
    with ExitStack() as ctx:
        def sb(tag, shape, dt=F32):
            return ctx.enter_context(nc.sbuf_tensor(f"{name}_{tag}", shape, dt))

        def ps(tag):
            return ctx.enter_context(nc.psum_tensor(f"{name}_{tag}", [P, BANK], F32))

        def sem(tag):
            return con.sem(f"{name}_{tag}")

        def two(make, tag, *args):
            return [make(f"{tag}{k}", *args) for k in range(2)]

        unit_int = two(sb, "unit_int", [1, 4], I32)
        store_int = sb("store_int", [1, 4], I32)
        unit_par = two(sb, "unit_par", [P, 4])
        idx = two(sb, "idx", [P, Q], I32)
        dst_ids = two(sb, "dst_ids", [P, Q], I32)
        rows_in = two(sb, "rows_in", [P, Q, row])
        own = two(sb, "own", [NB, row])
        out_sb = two(sb, "out_sb", [NB, out_cols])
        dst_local = sb("dst_local", [P, Q])
        onehot = two(sb, "onehot", [P, Q, NB])
        onehot_t = sb("onehot_t", [NB, CAP], BF16)
        mask = sb("mask", [P, Q, NB], BF16)
        masked = sb("masked", [P, heads, Q, NB])
        column_max = sb("column_max", [P, heads, NB])
        max_src = sb("max_src", [NB, heads])
        max_unit = sb("max_unit", [NB, heads])
        max_before = sb("max_before", [NB, heads])
        max_state = sb("max_state", [NB, heads])
        rescale = two(sb, "rescale", [NB, heads])
        node_vals = sb("node_vals", [NB, vals])
        rest = sb("rest", [NB, vals])
        node_split = sb("node_split", [NB, PARTS, vals], BF16)
        edge_vals = sb("edge_vals", [P, Q, vals])
        logits = sb("logits", [P, Q, heads])
        weights = sb("weights", [P, Q, heads])
        weighted = sb("weighted", [P, Q, heads * part])
        acc = sb("acc", [NB, heads * part])
        inverse = sb("inverse", [NB, heads])
        result = sb("result", [NB, heads * D])
        result_t = sb("result_t", [heads * D, NB])
        if first:
            edges = two(sb, "edges", [P, Q, D])
            pairs_t = sb("pairs_t", [P, Q // 2, P])
            edge_scores = sb("edge_scores", [P, Q, heads])
            scores_sum = sb("scores_sum", [P, Q, heads])
            w_cols = sb("w_cols", [P, heads * D])
            al = sb("al", [P, heads * D])
            wl = sb("wl", [P, heads])
            pair_w = sb("pair_w", [P, 2 * heads])
            w_heads = sb("w_heads", [P, D])
        else:
            bias_sb = sb("bias_sb", [NB, D])
            self_row = sb("self_row", [NB, part])
            self_max = sb("self_max", [NB, 1])
            if residual is not None:
                res_sb = two(sb, "res_sb", [NB, D])
            else:
                ext = extend_weights(nc, sb, "ext", *next_weights)

        ps_big = [ps(f"ps_big{g}") for g in range(CHUNKS)]
        ps_edge, ps_acc, ps_out = ps("ps_edge"), ps("ps_acc"), ps("ps_out")

        int_loaded, idx_loaded, meta_loaded, own_loaded, gathered, stored, edges_loaded, res_loaded = (
            two(sem, tag) for tag in ("int_loaded", "idx_loaded", "meta_loaded", "own_loaded",
                                      "gathered", "stored", "edges_loaded", "res_loaded"))
        rows_taken = two(sem, "rows_taken")
        store_int_loaded, w_loaded, w_made, state_set = (
            sem("store_int_loaded"), sem("w_loaded"), sem("w_made"), sem("state_set"))
        chain = sem("chain")
        tails_set, tail_gathered, tail_ready = sem("tails_set"), sem("tail_gathered"), two(sem, "tail_ready")
        passed_sp, passed_gp, passed_te = sem("passed_sp"), sem("passed_gp"), sem("passed_te")
        local_made, onehot_built, turned, onehot_copied, mask_made = (
            sem("local_made"), sem("onehot_built"), sem("turned"), sem("onehot_copied"), sem("mask_made"))
        pairs_turned, pairs_copied, scored, scores_copied, scores_ready = (
            sem("pairs_turned"), sem("pairs_copied"), sem("scored"), sem("scores_copied"), sem("scores_ready"))
        masked_made, columns_maxed, maxima_turned = (
            sem("masked_made"), sem("columns_maxed"), sem("maxima_turned"))
        split_made, expanded, logits_made, weights_made = (
            sem("split_made"), sem("expanded"), sem("logits_made"), sem("weights_made"))
        rows_weighted, aggregated = sem("rows_weighted"), sem("aggregated")
        result_made, result_turned, result_copied, projected, out_made = (
            sem("result_made"), sem("result_turned"), sem("result_copied"), sem("projected"), sem("out_made"))

        def last_pair(eng):
            last = eng.value_load(con.last_unit[0:1, 0:1], min_val=0, max_val=unit_ints.shape[0] - 3)
            return eng.snap(last // 2)

        def unit_pairs(eng):
            return eng.snap(last_pair(eng) + 1)

        with nc.Block() as block:
            @block.sync
            def _(sp):
                last = last_pair(sp)
                pairs = sp.snap(last + 1)

                def node0_of(ints):
                    return sp.value_load(ints[0:1, 0:1], min_val=0, max_val=table.shape[0] - NB)

                def load_window(tile, array, edge0, loaded):
                    main, tail = array[bass.ds(edge0, TAIL_AT)], array[bass.ds(edge0 + TAIL_AT, P)]
                    if len(array.shape) == 1:
                        sp.dma_start(tile[:, 0:Q - 1], main.rearrange("(p t) -> p t", p=P)).then_inc(loaded, 16)
                        sp.dma_start(tile[:, Q - 1:Q], tail.rearrange("(p t) -> p t", p=P),
                                     allow_slow_non_contiguous=True).then_inc(loaded, 16)
                    else:
                        sp.dma_start(tile[:, 0:Q - 1, :], main.rearrange("(p t) d -> p t d", p=P)
                                     ).then_inc(loaded, 16)
                        sp.dma_start(tile[:, Q - 1, :], tail).then_inc(loaded, 16)

                def wait_used(sem, value, wait):
                    if wait:
                        wait_apart(sp, sem, value, passed_sp)

                def load_unit(u, h, k, wait):
                    wait_used(gathered[h], 16 * (Q - 1) * k, wait)
                    wait_used(tail_ready[h], k, wait)
                    sp.dma_start(unit_int[h][:, :], unit_ints[bass.ds(u, 1), :]).then_inc(int_loaded[h], 16)
                    wait_apart(sp, int_loaded[h], 16 * k + 16, passed_sp)
                    node0 = node0_of(unit_int[h])
                    edge0 = sp.value_load(unit_int[h][0:1, 1:2], min_val=0, max_val=src.shape[0] - CAP)
                    load_window(idx[h], src, edge0, idx_loaded[h])
                    wait_used(onehot_built, 2 * k + h - 1, wait)
                    load_window(dst_ids[h], dst, edge0, meta_loaded[h])
                    wait_used(rows_weighted, 2 * k + h - 1, wait)
                    sp.dma_start(unit_par[h][:, :], unit_floats[bass.ds(u, 1), :].to_broadcast([P, 4])
                                 ).then_inc(meta_loaded[h], 16)
                    if first:
                        load_window(edges[h], edge_attr, edge0, edges_loaded[h])
                    sp.dma_start(own[h][:, :], table[bass.ds(node0, NB), :]).then_inc(own_loaded[h], 16)

                def load_residual(n, h):
                    if residual is not None:
                        node0 = node0_of(unit_int[h])
                        if not (isinstance(n, int) and n == 0):
                            wait_apart(sp, out_made, n, passed_sp)
                        sp.dma_start(res_sb[h][:, :], residual[bass.ds(node0, NB), :]
                                     ).then_inc(res_loaded[h], 16)

                def store(u, h, k):
                    sp.dma_start(store_int[:, :], unit_ints[bass.ds(u, 1), :]).then_inc(store_int_loaded, 16)
                    wait_apart(sp, store_int_loaded, 16 * u + 16, passed_sp)
                    node0 = node0_of(store_int)
                    wait_apart(sp, stored[1 - h], 16 * k + 32 + 16 * h, passed_sp)
                    wait_apart(sp, out_made, u + OUT_LAG, passed_sp)
                    sp.dma_start(out[bass.ds(node0, NB), :], out_sb[h][:, :]).then_inc(stored[h], 16)

                if first:
                    for half in range(2):
                        sp.dma_start(w_cols[half * D:(half + 1) * D, :], w_out).then_inc(w_loaded, 16)
                        sp.dma_start(w_heads[half * D:(half + 1) * D, :], w_out[:, half * D:(half + 1) * D]
                                     ).then_inc(w_loaded, 16)
                    sp.dma_start(al[:, :], attn_l.rearrange("h d -> (h d)").partition_broadcast(P)
                                 ).then_inc(w_loaded, 16)
                else:
                    sp.dma_start(bias_sb[:, :], bias.partition_broadcast(NB)).then_inc(w_loaded, 16)
                    if next_weights:
                        load_extended(sp, ext, *next_weights, w_loaded)
                for h in range(2):
                    sp.sem_inc(stored[h], 32)
                sp.sem_inc(res_loaded[1], 16)
                load_unit(0, 0, 0, False)
                load_unit(1, 1, 0, False)
                for h in range(2):
                    load_residual(h, h)
                    load_unit(2 + h, h, 1, True)
                with sp.Fori(0, last) as i:
                    for h in range(2):
                        n = sp.snap(2 * i + 2 + h)
                        load_residual(n, h)
                        load_unit(n + 2, h, i + 2, True)
                        store(sp.snap(2 * i + h), h, i)
                for h in range(2):
                    store(sp.snap(2 * last + h), h, last)
                for h in range(2):
                    wait_apart(sp, idx_loaded[h], 32 * pairs + 32, passed_sp)
                    wait_apart(sp, meta_loaded[h], 48 * pairs + 48, passed_sp)
                    wait_apart(sp, own_loaded[h], 16 * pairs + 16, passed_sp)
                    if first:
                        wait_apart(sp, edges_loaded[h], 32 * pairs + 32, passed_sp)
                    wait_apart(sp, stored[h], 16 * pairs + 32, passed_sp)

            @block.gpsimd
            def _(gp):
                pairs = unit_pairs(gp)

                def gather(h, t, done):
                    gp.indirect_dma_start(rows_in[h][:, t, :], None, table[:, :],
                                          bass.IndirectOffsetOnAxis(ap=idx[h][:, t:t + 1], axis=0)
                                          ).then_inc(done, 16)

                for h in range(2):
                    gp.memset(rows_in[h][:, Q - 1, :], 0.0).then_inc(tails_set, 1)
                gp.wait_ge(tails_set, 2)
                with gp.Fori(0, pairs) as i:
                    for h in range(2):
                        gp.wait_ge(rows_taken[h], i + 1)
                        wait_apart(gp, idx_loaded[h], 32 * i + 32, passed_gp)
                        has_tail = gp.value_load(unit_int[h][0:1, 2:3], min_val=0, max_val=1)
                        tails = gp.value_load(unit_int[h][0:1, 3:4], min_val=1, max_val=unit_ints.shape[0])
                        with gp.If(has_tail > 0):
                            gather(h, Q - 1, tail_gathered)
                        for t in range(Q - 1):
                            gather(h, t, gathered[h])
                        with gp.If(has_tail > 0):
                            wait_apart(gp, tail_gathered, 16 * tails, passed_gp)
                        gp.sem_inc(tail_ready[h], 1)

            @block.vector
            def _(ve):
                pairs = unit_pairs(ve)
                STEPS = 20 if first else 23

                ve.wait_ge(w_loaded, 5 * 16 if first else 4 * 16 if next_weights else 16)
                if first:
                    step = own_steps(ve, w_made)
                    step(ve.tensor_tensor(al[:, :], al[:, :], w_cols[:, :], ALU.mult))
                    step(ve.tensor_reduce(wl[:, :], al[:, :].rearrange("p (h d) -> p h d", h=heads), AX.X,
                                          ALU.add))
                    step(ve.memset(pair_w[:, :], 0.0))
                    step(ve.tensor_copy(pair_w[0:D, 0:heads], wl[0:D, :]))
                    step(ve.tensor_copy(pair_w[D:P, heads:2 * heads], wl[D:P, :]))
                elif next_weights:
                    make_extended(ve, own_steps(ve, w_made), ext)
                step = own_steps(ve, state_set)
                step(ve.memset(acc[:, :], 0.0))
                step(ve.memset(rescale[1][:, :], 0.0))
                step(ve.memset(max_state[:, :], 0.0))
                step(ve.memset(ps_acc[0:NB, 0:heads * part], 0.0))
                if residual is not None:
                    step(ve.memset(res_sb[1][:, :], 0.0))
                step(ve.memset(ps_out[:, :], 0.0))
                ve.sem_inc(result_turned, 1)

                def build_onehot(n, k, h):
                    ve.wait_ge(meta_loaded[h], 48 * k + 48)
                    ve.tensor_scalar(dst_local[:, :], dst_ids[h][:, :], unit_par[h][:, 0:1], None,
                                     ALU.subtract).then_inc(local_made, 1)
                    ve.wait_ge(local_made, n + 1)
                    ve.tensor_tensor(onehot[h][:, :, :], bcast(con.iota_nodes[:, :], 1, Q),
                                     bcast(dst_local[:, :], 2, NB), ALU.is_equal).then_inc(onehot_built, 1)

                def finish(i, h, n, step):
                    ve.wait_ge(weights_made, 2 * n + 2)
                    for hd in range(heads):
                        span = slice(hd * part, (hd + 1) * part)
                        step(ve.scalar_tensor_tensor(acc[:, span], acc[:, span], rescale[1 - h][:, hd:hd + 1],
                                                     ps_acc[0:NB, span], ALU.mult, ALU.add))
                    step(ve.tensor_scalar(inverse[:, :], acc[:, D::part], 1e-16, None, ALU.add))
                    step(ve.reciprocal(inverse[:, :], inverse[:, :]))
                    if first:
                        step(ve.tensor_scalar(result[:, 0:D], acc[:, 0:D], inverse[:, 0:1], None, ALU.mult))
                        ve.tensor_scalar(result[:, D:2 * D], acc[:, part:part + D], inverse[:, 1:2], None,
                                         ALU.mult).then_inc(result_made, 1)
                        return
                    ve.scalar_tensor_tensor(result[:, :], acc[:, 0:D], inverse[:, 0:1], bias_sb[:, :],
                                            ALU.mult, ALU.add).then_inc(result_made, 1)
                    if residual is not None:
                        ve.wait_ge(result_made, n + 1)
                        ve.wait_ge(res_loaded[1 - h], 16 * i + 16)
                        ve.wait_ge(stored[1 - h], 16 * i + 16 + 16 * h)
                        ve.tensor_tensor(out_sb[1 - h][:, :], result[:, :], res_sb[1 - h][:, :], ALU.add
                                         ).then_inc(out_made, 1)

                def begin(h, step):
                    carries, begins, low = (unit_par[h][0:NB, k:k + 1] for k in (1, 2, 3))
                    step(ve.tensor_copy(node_vals[:, 0:heads], own[h][:, D + heads:row]))
                    if first:
                        step(ve.tensor_scalar(max_before[:, :], max_state[:, :], carries, low, ALU.mult, ALU.add))
                        return
                    step(ve.tensor_tensor(self_max[:, :], own[h][:, D:D + 1], own[h][:, D + 1:D + 2], ALU.add))
                    step(ve.scalar_tensor_tensor(self_max[:, :], self_max[:, :], SLOPE, self_max[:, :],
                                                 ALU.mult, ALU.max))
                    step(ve.tensor_scalar(self_max[:, :], self_max[:, :], begins, None, ALU.mult))
                    step(ve.scalar_tensor_tensor(max_before[:, :], max_state[:, :], carries, self_max[:, :],
                                                 ALU.mult, ALU.add))

                def begin_sums(h, step):
                    carries, begins = (unit_par[h][0:NB, k:k + 1] for k in (1, 2))
                    ve.tensor_scalar(self_row[:, 0:D], own[h][:, 0:D], begins, None, ALU.mult)
                    step(ve.tensor_copy(self_row[:, D:part], begins))
                    step(ve.scalar_tensor_tensor(acc[:, :], acc[:, :], carries, self_row[:, :],
                                                 ALU.mult, ALU.add))

                def weigh(i, h, n, k_next, step):
                    ve.wait_ge(gathered[h], 16 * (Q - 1) * i + 16 * (Q - 1))
                    ve.wait_ge(tail_ready[h], i + 1)
                    ve.wait_ge(own_loaded[h], 16 * i + 16)
                    if first:
                        ve.wait_ge(scores_copied, n + 1)
                        ve.wait_ge(edges_loaded[h], 32 * i + 32)
                        ve.tensor_tensor(scores_sum[:, :, :], edge_scores[:, :, :], rows_in[h][:, :, D:D + heads],
                                         ALU.add).then_inc(scores_ready, 1)
                        ve.tensor_tensor(edges[h][:, :, :], edges[h][:, :, :], rows_in[h][:, :, 0:D], ALU.add
                                         ).then_inc(rows_taken[h], 1)
                    begin(h, step)
                    if not first:
                        ve.wait_ge(aggregated, n + 1)
                        build_onehot(n + 1, k_next, 1 - h)
                        finish(i, h, n, step)
                        begin_sums(h, step)
                    for hd in range(heads):
                        ve.wait_ge(masked_made, heads * n + hd + 1)
                        ve.tensor_reduce(column_max[:, hd, :], masked[:, hd, :, :].rearrange("p t n -> p n t"),
                                         AX.X, ALU.max).then_inc(columns_maxed, 1)
                        if first and hd == 0:
                            ve.wait_ge(aggregated, n + 1)
                            build_onehot(n + 1, k_next, 1 - h)
                    ve.wait_ge(maxima_turned, n + 1)
                    step(ve.tensor_reduce(max_src[:, :], ps_acc[0:NB, MAX_AT:MAX_AT + heads * P]
                                          .rearrange("p (h e) -> p h e", h=heads), AX.X, ALU.max))
                    step(ve.tensor_tensor(max_unit[:, :], node_vals[:, 0:heads], max_src[:, :], ALU.add))
                    step(ve.scalar_tensor_tensor(max_unit[:, :], max_unit[:, :], SLOPE, max_unit[:, :],
                                                 ALU.mult, ALU.max))
                    step(ve.tensor_tensor(node_vals[:, heads:vals], max_before[:, :], max_unit[:, :], ALU.max))
                    step(ve.tensor_copy(node_split[:, 0, :], node_vals[:, :]))
                    step(ve.tensor_tensor(rest[:, :], node_vals[:, :], node_split[:, 0, :], ALU.subtract))
                    step(ve.tensor_copy(node_split[:, 1, :], rest[:, :]))
                    ve.tensor_tensor(node_split[:, 2, :], rest[:, :], node_split[:, 1, :], ALU.subtract
                                     ).then_inc(split_made, 1)
                    step(ve.tensor_tensor(rescale[h][:, :], max_before[:, :], node_vals[:, heads:vals],
                                          ALU.subtract))
                    step(ve.tensor_copy(max_state[:, :], node_vals[:, heads:vals]))
                    if first:
                        finish(i, h, n, step)
                    ve.wait_ge(expanded, n + 1)
                    step(ve.tensor_reduce(edge_vals[:, :, :], ps_edge[:, 0:Q * PARTS * vals]
                                          .rearrange("p (t s k) -> p t k s", s=PARTS, k=vals), AX.X, ALU.add))
                    scores = scores_sum[:, :, :] if first else rows_in[h][:, :, D:D + 1]
                    step(ve.tensor_tensor(logits[:, :, :], scores, edge_vals[:, :, 0:heads], ALU.add))
                    step(ve.scalar_tensor_tensor(logits[:, :, :], logits[:, :, :], SLOPE, logits[:, :, :],
                                                 ALU.mult, ALU.max))
                    step(ve.tensor_tensor(logits[:, :, :], logits[:, :, :], edge_vals[:, :, heads:vals],
                                          ALU.subtract))
                    ve.tensor_scalar(logits[:, :, :], logits[:, :, :], 0.0, None, ALU.min).then_inc(logits_made, 1)
                    ve.wait_ge(weights_made, 2 * n + 3)
                    rows = edges[h] if first else rows_in[h]
                    for hd in range(heads):
                        ins = ve.tensor_tensor(weighted[:, :, hd * part:hd * part + D], rows[:, :, 0:D],
                                               bcast(weights[:, :, hd], 2, D), ALU.mult)
                    if not first:
                        ins.then_inc(rows_taken[h], 1)
                    ve.tensor_copy(weighted[:, :, D::part], weights[:, :, :]).then_inc(rows_weighted, 1)

                for h in range(2):
                    ve.sem_inc(rows_taken[h], 1)
                build_onehot(0, 0, 0)
                with ve.Fori(0, pairs) as i:
                    for h in range(2):
                        n = ve.snap(2 * i + h)
                        step = own_steps(ve, chain, ve.snap(n * STEPS))
                        weigh(i, h, n, i + h, step)
                        assert step.taken() == STEPS, step.taken()
                n = ve.snap(2 * pairs)
                ve.wait_ge(aggregated, n + 1)
                finish(pairs, 0, n, own_steps(ve, chain, ve.snap(n * STEPS)))

            @block.scalar
            def _(ac):
                pairs = unit_pairs(ac)

                def copy_pairs(n):
                    ac.wait_ge(pairs_turned, n + 1)
                    for j0 in range(0, Q // 2, GROUP):
                        j1 = min(j0 + GROUP, Q // 2)
                        ins = ac.activation(
                            pairs_t[:, j0:j1, :],
                            ps_big[j0 // GROUP][:, 0:(j1 - j0) * P].rearrange("p (j e) -> p j e", e=P),
                            ACT.Copy)
                    ins.then_inc(pairs_copied, 1)

                def copy_scores(n):
                    ac.wait_ge(scored, n + 1)
                    ac.activation(edge_scores[:, :, :], ps_out[:, SCORE_AT:SCORE_AT + Q * heads]
                                  .rearrange("p (t k) -> p t k", k=heads), ACT.Copy
                                  ).then_inc(scores_copied, 1)

                def make_mask(n, h):
                    ac.wait_ge(onehot_built, n + 1)
                    ac.activation(mask[:, :, :], onehot[h][:, :, :], ACT.Copy, bias=-BIG, scale=BIG
                                  ).then_inc(mask_made, 1)

                def copy_result(n):
                    if residual is None:
                        ac.wait_ge(result_turned, n + 1)
                        ac.activation(result_t[:, :], ps_out[0:heads * D, 0:NB], ACT.Copy if first else ACT.Relu
                                      ).then_inc(result_copied, 1)

                def copy_out(i, h, n):
                    if residual is None:
                        ac.wait_ge(projected, n + 1)
                        ac.wait_ge(stored[h], 16 * i + 16)
                        ac.activation(out_sb[h][:, :], ps_out[0:NB, PROJ_AT:PROJ_AT + out_cols], ACT.Copy,
                                      scale=1.0 / heads).then_inc(out_made, 1)

                ac.sem_inc(weights_made, 1)
                ac.wait_ge(state_set, 2)
                ac.activation(rescale[1][:, :], rescale[1][:, :], ACT.Exp).then_inc(weights_made, 1)
                if first:
                    copy_pairs(0)
                    copy_scores(0)
                make_mask(0, 0)
                with ac.Fori(0, pairs) as i:
                    for h in range(2):
                        n = ac.snap(2 * i + h)
                        ac.wait_ge(mask_made, n + 1)
                        if first:
                            ac.wait_ge(scores_ready, n + 1)
                        else:
                            ac.wait_ge(gathered[h], 16 * (Q - 1) * i + 16 * (Q - 1))
                            ac.wait_ge(tail_ready[h], i + 1)
                        for hd in range(heads):
                            for t in range(Q):
                                score = scores_sum[:, t, hd:hd + 1] if first else rows_in[h][:, t, D:D + 1]
                                ins = ac.activation(masked[:, hd, t, :], mask[:, t, :], ACT.Identity, bias=score)
                            ins.then_inc(masked_made, 1)
                        ac.wait_ge(turned, n + 1)
                        for g in range(CHUNKS):
                            cols = len(chunk_cols(g)) * P
                            ins = ac.activation(onehot_t[:, g * BANK:g * BANK + cols], ps_big[g][0:NB, 0:cols],
                                                ACT.Copy)
                        ins.then_inc(onehot_copied, 1)
                        copy_result(n)
                        if first:
                            copy_pairs(n + 1)
                        if not first:
                            ac.wait_ge(masked_made, n + 1)
                            make_mask(n + 1, 1 - h)
                        ac.wait_ge(logits_made, n + 1)
                        ac.activation(weights[:, :, :], logits[:, :, :], ACT.Exp).then_inc(weights_made, 1)
                        ac.activation(rescale[h][:, :], rescale[h][:, :], ACT.Exp).then_inc(weights_made, 1)
                        if first:
                            make_mask(n + 1, 1 - h)
                            ac.wait_ge(scored, n + 2)
                        copy_out(i, h, n)
                        if first:
                            copy_scores(n + 1)
                for h in range(2):
                    n = ac.snap(2 * pairs + h)
                    copy_result(n)
                    copy_out(pairs, h, n)

            @block.tensor
            def _(te):
                pairs = unit_pairs(te)

                def turn_pairs(n, k, h):
                    te.wait_ge(edges_loaded[h], 32 * k + 32)
                    for j in range(Q // 2):
                        ins = te.transpose(ps_big[j // GROUP][:, j % GROUP * P:(j % GROUP + 1) * P],
                                           edges[h][:, 2 * j:2 * j + 2, :].rearrange("p t d -> p (t d)"),
                                           con.ident[:, :])
                    ins.then_inc(pairs_turned, 1)

                def score_pairs(n):
                    te.wait_ge(pairs_copied, n + 1)
                    for j in range(Q // 2):
                        at = SCORE_AT + 2 * heads * j
                        ins = te.matmul(ps_out[:, at:at + 2 * heads], pairs_t[:, j, :], pair_w[:, :])
                    ins.then_inc(scored, 1)

                def turn_onehot(n, h):
                    te.wait_ge(onehot_built, n + 1)
                    for t in range(Q):
                        ins = te.transpose(ps_big[t // GROUP][0:NB, t % GROUP * P:(t % GROUP + 1) * P],
                                           onehot[h][:, t, :], con.ident[:, :])
                    ins.then_inc(turned, 1)

                def project(n):
                    if residual is None:
                        te.wait_ge(result_copied, n + 1)
                        te.matmul(ps_out[0:NB, PROJ_AT:PROJ_AT + out_cols], result_t[:, :],
                                  w_heads[:, :] if first else ext[0][:, :]).then_inc(projected, 1)

                def turn_result(n):
                    if residual is None:
                        te.wait_ge(out_made, n + 1)
                        wait_apart(te, result_made, n + 1, passed_te)
                        te.transpose(ps_out[0:heads * D, 0:NB], result[:, :], con.ident[0:NB, 0:NB]
                                     ).then_inc(result_turned, 1)

                te.sem_inc(aggregated, 1)
                te.wait_ge(result_turned, 1)
                if first:
                    te.wait_ge(w_made, 5)
                    turn_pairs(0, 0, 0)
                    score_pairs(0)
                elif next_weights:
                    te.wait_ge(w_made, 4)
                turn_onehot(0, 0)
                with te.Fori(0, pairs) as i:
                    for h in range(2):
                        n = te.snap(2 * i + h)
                        te.wait_ge(onehot_copied, n + 1)
                        if first:
                            turn_pairs(n + 1, i + h, 1 - h)
                        te.wait_ge(columns_maxed, heads * n + heads)
                        for hd in range(heads):
                            ins = te.transpose(ps_acc[0:NB, MAX_AT + hd * P:MAX_AT + (hd + 1) * P],
                                               column_max[:, hd, :], con.ident[:, :])
                        ins.then_inc(maxima_turned, 1)
                        te.wait_ge(split_made, n + 1)
                        for t in range(Q):
                            ins = te.matmul(ps_edge[:, PARTS * vals * t:PARTS * vals * (t + 1)],
                                            onehot_t[:, t * P:(t + 1) * P],
                                            node_split[:, :, :].rearrange("p s k -> p (s k)"))
                        ins.then_inc(expanded, 1)
                        project(n)
                        if first:
                            score_pairs(n + 1)
                        else:
                            turn_onehot(n + 1, 1 - h)
                        if first:
                            te.wait_ge(scores_copied, n + 2)
                        turn_result(n)
                        te.wait_ge(rows_weighted, n + 1)
                        for t in range(Q):
                            ins = te.matmul(ps_acc[0:NB, 0:heads * part], onehot[h][:, t, :], weighted[:, t, :],
                                            start=t == 0, stop=t == Q - 1)
                        ins.then_inc(aggregated, 1)
                        if first:
                            turn_onehot(n + 1, 1 - h)
                n = te.snap(2 * pairs)
                project(n)
                turn_result(n)
                project(te.snap(n + 1))


def graph_network(nc, n_nodes, n_edges, x, src, dst, edge_attr, w0, attn_l, attn_r, gamma, beta, w1, a1s,
                  a1d, b1, w2, a2s, a2d, b2, w3, a3s, a3d, b3, out):
    blocks = n_nodes // NB
    rounds = -(-n_edges // CAP)
    grid = -(-(blocks * rounds + 2) // P) * P

    def dram(name, shape, dt=F32):
        return nc.dram_tensor(name, shape, dt).ap()
    unit_ints, unit_floats = dram("unit_ints", (grid, 4), I32), dram("unit_floats", (grid, 4))
    h_in = dram("h_in", (n_nodes, D + 4))
    h_heads, x_mid = dram("h_heads", (n_nodes, D)), dram("x_mid", (n_nodes, D))
    tables = [dram(f"table{k}", (n_nodes, ROW)) for k in range(3)]
    units = unit_ints, unit_floats
    with ExitStack() as ctx:
        con = Constants(nc, ctx)
        list_units(nc, con, dst, unit_ints, unit_floats, n_nodes, n_edges)
        con.end_phase()
        first_nodes(nc, con, x, attn_l, attn_r, w0, h_in, 2, n_nodes)
        con.end_phase()
        attention_layer(nc, con, "heads", units, src, dst, h_in, h_heads,
                        edge_attr=edge_attr, attn_l=attn_l, w_out=w0)
        con.end_phase()
        middle_nodes(nc, con, x, h_heads, gamma, beta, w1, a1s, a1d, x_mid, tables[0], n_nodes)
        plain = [(b1, (w2, a2s, a2d)), (b2, (w3, a3s, a3d)), (b3, None)]
        for k, (bias, following) in enumerate(plain):
            con.end_phase()
            attention_layer(nc, con, f"plain{k}", units, src, dst, tables[k],
                            tables[k + 1] if following else out, bias=bias, next_weights=following,
                            residual=None if following else x_mid)


NAMES = ["x", "src", "dst", "edge_attr_64", "L0_gnn_W", "L0_gnn_attn_l", "L0_gnn_attn_r", "L0_gnn_bn_gamma",
         "L0_gnn_bn_beta", "L1_gnn_W1", "L1_gnn_a1s", "L1_gnn_a1d", "L1_gnn_b1", "L1_gnn_W2", "L1_gnn_a2s",
         "L1_gnn_a2d", "L1_gnn_b2", "L1_gnn_W3", "L1_gnn_a3s", "L1_gnn_a3d", "L1_gnn_b3"]


def kernel(**inputs):
    import numpy as np
    import concourse.bacc as bacc
    from concourse.bass_utils import run_bass_kernel_spmd

    arrays = {name: np.ascontiguousarray(inputs[name]) for name in NAMES}
    n_nodes, n_edges = arrays["x"].shape[0], arrays["src"].shape[0]
    for name, fill in (("src", 0), ("dst", 2 * n_nodes), ("edge_attr_64", 0)):
        a = arrays[name]
        arrays[name] = np.concatenate([a, np.full((CAP,) + a.shape[1:], fill, a.dtype)])
    nc = bacc.Bacc("TRN2", target_bir_lowering=False, num_devices=1)
    args = [nc.dram_tensor("in_" + name, arrays[name].shape, mybir.dt.from_np(arrays[name].dtype),
                           kind="ExternalInput").ap() for name in NAMES]
    out = nc.dram_tensor("out", (n_nodes, D), F32, kind="ExternalOutput").ap()
    graph_network(nc, n_nodes, n_edges, *args, out)
    r = run_bass_kernel_spmd(nc, [{"in_" + name: arrays[name] for name in NAMES}], core_ids=[0])
    return r.results[0]["out"]
```

```python
from contextlib import ExitStack

import concourse.bass as bass
from concourse import mybir

F32 = mybir.dt.float32
I32 = mybir.dt.int32
BF16 = mybir.dt.bfloat16
ALU = mybir.AluOpType
ACT = mybir.ActivationFunctionType
AX = mybir.AxisListType

P = 128
D = 64
NB = 125
CUTS = 5
Q = 18
CAP = P * Q
TAIL_AT = P * (Q - 1)
GROUP = 4
BANK = 512
CHUNKS = -(-Q // GROUP)
EARLY = 12
SLOPE = 0.2
EPS = 1e-5
BIG = float(2 ** 80)
ROW = D + 2


def bcast(ap, axis, count):
    wide = ap.unsqueeze(axis)
    shape = list(wide.shape)
    shape[axis] = count
    return wide.to_broadcast(shape)


def chunk_cols(g):
    return range(g * GROUP, min((g + 1) * GROUP, Q))


class Constants:

    def __init__(self, nc, ctx):
        def sb(name, shape, dt=F32):
            return ctx.enter_context(nc.sbuf_tensor(name, shape, dt))
        self.ident = sb("ident", [P, P])
        self.ones = sb("ones", [P, P])
        self.iota_nodes = sb("iota_nodes", [P, NB])
        self.eps = sb("eps", [P, 1])
        self.last_unit = sb("last_unit", [1, 1], I32)
        self.nc = nc
        self.taken = []

    def sem(self, name):
        self.taken.append(self.nc.alloc_semaphore(name=name))
        return self.taken[-1]

    def end_phase(self):
        self.nc.clear_and_free_semaphores(self.taken)
        self.nc.all_engine_barrier()
        self.taken = []


def wait_apart(eng, sem, value, passed):
    eng.wait_ge(sem, value)
    eng.sem_inc(passed, 1)


def own_steps(eng, chain, base=0):
    count = {}

    def step(ins, signal=None):
        signal, before = (chain, base) if signal is None else (signal, 0)
        count[id(signal)] = count.get(id(signal), 0) + 1
        ins.then_inc(signal, 1)
        eng.wait_ge(signal, before + count[id(signal)])
    step.taken = lambda: count[id(chain)]
    return step


def list_units(nc, con, dst, unit_ints, unit_floats, n_nodes, n_edges, make_nodes):
    blocks = n_nodes // NB
    rows = NB
    row_len = n_edges // rows
    rounds = -(-n_edges // CAP)
    per_part = unit_ints.shape[0] // P
    assert 3 * (per_part + 1) <= BANK and blocks < P and rows <= P
    with ExitStack() as ctx:
        def sb(name, shape, dt=F32):
            return ctx.enter_context(nc.sbuf_tensor(name, shape, dt))

        def ps(name):
            return ctx.enter_context(nc.psum_tensor(name, [P, BANK], F32))

        nodes = make_nodes(ctx)
        dst_rows = sb("dst_rows", [rows, row_len], I32)
        dst_next = sb("dst_next", [rows, row_len], I32)
        falls = sb("falls", [rows, row_len])
        fallen = sb("fallen", [rows, 1])
        first_dst = sb("first_dst", [rows, 1])
        thr_row = sb("thr_row", [rows, blocks + 1])
        thr_col = sb("thr_col", [blocks + 1, 1])
        below = sb("below", [rows, blocks + 1])
        row_of = sb("row_of", [blocks + 1, 1])
        row_of_i = sb("row_of_i", [blocks + 1, 1], I32)
        edge_row = sb("edge_row", [blocks + 1, row_len], I32)
        edge_row_f = sb("edge_row_f", [blocks + 1, row_len])
        inner = sb("inner", [blocks + 1, 1])
        is_sorted = sb("is_sorted", [blocks + 1, 1])
        all_edges = sb("all_edges", [blocks + 1, 1])
        start = sb("start", [blocks + 1, 1])
        step_mat = sb("step_mat", [blocks + 1, blocks])
        cum_mat = sb("cum_mat", [blocks, blocks])
        size = sb("size", [blocks, 1])
        caps = sb("caps", [blocks, rounds])
        over = sb("over", [blocks, rounds])
        units_extra = sb("units_extra", [blocks, 1])
        steps = sb("steps", [blocks, 3])
        ends = sb("ends", [blocks, 1])
        unit_row = sb("unit_row", [blocks, (P + 1) * per_part])
        unit_id = sb("unit_id", [P, per_part + 1])
        sums = sb("sums", [P, per_part + 1, 3])
        rnd = sb("rnd", [P, per_part + 1])
        edge0 = sb("edge0", [P, per_part + 1])
        always = sb("always", [P, 1])
        tail = sb("tail", [P, per_part])
        tails = [sb(f"tails{k}", [P, per_part]) for k in range(2)]
        earlier = sb("earlier", [P, P])
        ints = sb("ints", [P, per_part, 4], I32)
        floats = sb("floats", [P, per_part, 4])
        ps_sums, ps_columns = ps("ps_sums"), ps("ps_columns")
        ps_before, ps_falls, ps_steps, ps_ends, ps_total, ps_tails = (ps_columns[:, k:k + 1] for k in range(6))

        sem = con.sem
        dst_loaded, rows_gathered, stored = sem("dst_loaded"), sem("rows_gathered"), sem("list_stored")
        const_made, chain = sem("const_made"), sem("list_chain")
        below_made, falls_counted, row_known, starts_known = (
            sem("below_made"), sem("falls_counted"), sem("row_known"), sem("starts_known"))
        tails_counted, tails_summed = sem("tails_counted"), sem("tails_summed")
        units_known, past_made, list_made = sem("units_known"), sem("past_made"), sem("list_made")
        before_summed, falls_summed, steps_summed, ends_summed, units_summed = (
            sem("before_summed"), sem("falls_summed"), sem("steps_summed"), sem("ends_summed"),
            sem("units_summed"))
        MADE = 15

        with nc.Block() as block:
            @block.sync
            def _(sp):
                def rows_of(off):
                    return dst[off:off + n_edges].rearrange("(p j) -> p j", p=rows)
                sp.dma_start(dst_rows[:, :], rows_of(0)).then_inc(dst_loaded, 16)
                sp.dma_start(dst_next[:, :], rows_of(1)).then_inc(dst_loaded, 16)
                nodes.load(sp)
                sp.wait_ge(list_made, 6)
                sp.dma_start(unit_ints.rearrange("(p c) k -> p c k", p=P), ints[:, :, :]).then_inc(stored, 16)
                sp.dma_start(unit_floats.rearrange("(p c) k -> p c k", p=P), floats[:, :, :]).then_inc(stored, 16)
                nodes.store(sp)
                sp.wait_ge(stored, 32)

            @block.scalar
            def _(ac):
                nodes.scalar(ac)

            @block.gpsimd
            def _(gp):
                def iota(out, pattern, base=0, channel=0):
                    gp.iota(out, pattern, base=base, channel_multiplier=channel,
                            allow_small_or_imprecise_dtypes=True).then_inc(const_made, 1)

                def where(out, compare, fill, base, n, column=-1):
                    gp.affine_select(out=out, in_=out, compare_op=compare, fill=fill, base=base,
                                     pattern=[[column, n]], channel_multiplier=-column
                                     ).then_inc(const_made, 1)
                iota(thr_row[:, :], [[NB, blocks + 1]])
                iota(thr_col[:, :], [[0, 1]], channel=NB)
                iota(con.iota_nodes[:, :], [[1, NB]])
                iota(caps[:, :], [[CAP, rounds]], base=CAP)
                iota(unit_id[:, :], [[1, per_part + 1]], channel=per_part)
                gp.memset(con.ident[:, :], 0.0).then_inc(const_made, 1)
                gp.memset(step_mat[:, :], 0.0).then_inc(const_made, 1)
                gp.memset(cum_mat[:, :], 1.0).then_inc(const_made, 1)
                gp.memset(earlier[:, :], 1.0).then_inc(const_made, 1)
                gp.wait_ge(const_made, 9)
                where(con.ident[:, :], ALU.not_equal, 1.0, 0, P)
                where(step_mat[:, :], ALU.not_equal, 1.0, -1, blocks)
                where(cum_mat[:, :], ALU.is_ge, 0.0, 0, blocks, column=1)
                where(earlier[:, :], ALU.is_gt, 0.0, 0, P, column=1)
                gp.wait_ge(const_made, 13)
                where(step_mat[:, :], ALU.not_equal, -1.0, 0, blocks)
                iota(unit_row[:, :], [[1, (P + 1) * per_part]])
                gp.wait_ge(row_known, 1)
                gp.indirect_dma_start(edge_row[:, :], None, dst[0:n_edges].rearrange("(p j) -> p j", p=rows),
                                      bass.IndirectOffsetOnAxis(ap=row_of_i[:, 0:1], axis=0)
                                      ).then_inc(rows_gathered, 16)
                gp.wait_ge(rows_gathered, 16)

            @block.vector
            def _(ve):
                step = own_steps(ve, chain)
                step(ve.memset(con.ones[:, :], 1.0))
                step(ve.memset(con.eps[:, :], EPS))
                step(ve.memset(steps[:, 0:1], 1.0))
                ve.wait_ge(dst_loaded, 32)
                ve.wait_ge(const_made, MADE)
                step(ve.tensor_copy(first_dst[:, :], dst_rows[:, 0:1]))
                step(ve.tensor_scalar(below[:, :], thr_row[:, :], first_dst[:, 0:1], None, ALU.is_gt),
                     below_made)
                ve.wait_ge(before_summed, 1)
                step(ve.tensor_scalar(row_of[:, :], ps_before[0:blocks + 1, 0:1], -1.0, 0.0, ALU.add, ALU.max))
                step(ve.tensor_copy(row_of_i[:, :], row_of[:, :]), row_known)
                step(ve.tensor_tensor(falls[:, :], dst_rows[:, :], dst_next[:, :], ALU.is_gt))
                step(ve.tensor_reduce(fallen[:, :], falls[:, :], AX.X, ALU.add), falls_counted)
                ve.wait_ge(rows_gathered, 16)
                step(ve.tensor_copy(edge_row_f[:, :], edge_row[:, :]))
                step(ve.tensor_scalar(edge_row_f[:, :], edge_row_f[:, :], thr_col[:, 0:1], None, ALU.is_lt))
                step(ve.tensor_reduce(inner[:, :], edge_row_f[:, :], AX.X, ALU.add))
                ve.wait_ge(falls_summed, 1)
                step(ve.tensor_scalar(always[:, :], ps_falls[:, 0:1], 0.0, None, ALU.is_gt))
                step(ve.tensor_scalar(is_sorted[:, :], ps_falls[0:blocks + 1, 0:1], 0.0, None, ALU.is_equal))
                step(ve.scalar_tensor_tensor(start[:, :], row_of[:, :], float(row_len), inner[:, :],
                                             ALU.mult, ALU.add))
                step(ve.tensor_scalar(start[:, :], start[:, :], is_sorted[:, 0:1], None, ALU.mult), starts_known)
                step(ve.tensor_scalar(all_edges[:, :], is_sorted[:, :], float(-n_edges), float(n_edges),
                                      ALU.mult, ALU.add))
                ve.wait_ge(steps_summed, 1)
                step(ve.tensor_copy(steps[:, 2:3], ps_steps[0:blocks, 0:1]))
                step(ve.tensor_tensor(size[:, :], steps[:, 2:3], all_edges[0:blocks, :], ALU.add))
                step(ve.tensor_scalar(over[:, :], caps[:, :], size[:, 0:1], None, ALU.is_lt))
                step(ve.tensor_reduce(units_extra[:, :], over[:, :], AX.X, ALU.add))
                step(ve.tensor_scalar(steps[:, 1:2], units_extra[:, :], 1.0, None, ALU.add), units_known)
                ve.wait_ge(ends_summed, 1)
                step(ve.tensor_copy(ends[:, :], ps_ends[0:blocks, 0:1]))
                step(ve.tensor_scalar(con.last_unit[:, :], ps_total[0:1, 0:1], -1.0, None, ALU.add))
                step(ve.tensor_scalar(unit_row[:, :], unit_row[:, :], ends[:, 0:1], None, ALU.is_ge), past_made)
                nodes.vector(ve)
                ve.wait_ge(units_summed, 1)
                step(ve.tensor_copy(sums[:, :, :].rearrange("p c k -> p (c k)"), ps_sums[:, 0:3 * (per_part + 1)]))
                step(ve.tensor_tensor(rnd[:, :], unit_id[:, :], sums[:, :, 1], ALU.subtract))
                step(ve.scalar_tensor_tensor(edge0[:, :], rnd[:, :], float(CAP), sums[:, :, 2],
                                             ALU.mult, ALU.add))
                step(ve.tensor_scalar(edge0[:, :], edge0[:, :], float(n_edges), None, ALU.min))
                step(ve.tensor_scalar(floats[:, :, 0], sums[:, 0:per_part, 0], float(NB), None, ALU.mult))
                step(ve.tensor_scalar(floats[:, :, 1], rnd[:, 0:per_part], 0.0, None, ALU.is_gt))
                step(ve.tensor_tensor(tail[:, :], edge0[:, 1:per_part + 1], edge0[:, 0:per_part], ALU.subtract))
                step(ve.tensor_scalar(tail[:, :], tail[:, :], float(TAIL_AT), always[:, 0:1], ALU.is_gt, ALU.max))
                step(ve.tensor_copy(tails[0][:, :], tail[:, :]))
                now, reach = 0, 1
                while reach < per_part:
                    step(ve.tensor_copy(tails[1 - now][:, 0:reach], tails[now][:, 0:reach]))
                    step(ve.tensor_tensor(tails[1 - now][:, reach:], tails[now][:, reach:],
                                          tails[now][:, 0:per_part - reach], ALU.add))
                    now, reach = 1 - now, 2 * reach
                step(ve.tensor_copy(always[:, :], tails[now][:, per_part - 1:per_part]), tails_counted)
                ve.wait_ge(tails_summed, 1)
                step(ve.tensor_scalar(always[:, :], ps_tails[:, 0:1], 0.0, None, ALU.add))
                step(ve.tensor_scalar(tails[now][:, :], tails[now][:, :], always[:, 0:1], 1.0, ALU.add, ALU.max))
                step(ve.tensor_copy(ints[:, :, 0], floats[:, :, 0]), list_made)
                step(ve.tensor_copy(ints[:, :, 1], edge0[:, 0:per_part]), list_made)
                step(ve.tensor_copy(ints[:, :, 2], tail[:, :]), list_made)
                step(ve.tensor_copy(ints[:, :, 3], tails[now][:, :]), list_made)
                step(ve.tensor_scalar(floats[:, :, 2], floats[:, :, 1], -1.0, 1.0, ALU.mult, ALU.add), list_made)
                step(ve.tensor_scalar(floats[:, :, 3], floats[:, :, 1], BIG, -BIG, ALU.mult, ALU.add), list_made)

            @block.tensor
            def _(te):
                te.wait_ge(below_made, 1)
                te.matmul(ps_before[0:blocks + 1, 0:1], below[:, :], con.ones[0:rows, 0:1]).then_inc(before_summed, 1)
                te.wait_ge(falls_counted, 1)
                te.matmul(ps_falls[:, 0:1], con.ones[0:rows, :], fallen[:, :]).then_inc(falls_summed, 1)
                te.wait_ge(starts_known, 1)
                te.matmul(ps_steps[0:blocks, 0:1], step_mat[:, :], start[:, :]).then_inc(steps_summed, 1)
                te.wait_ge(units_known, 1)
                te.matmul(ps_total[0:1, 0:1], steps[:, 1:2], con.ones[0:blocks, 0:1])
                te.matmul(ps_ends[0:blocks, 0:1], cum_mat[:, :], steps[:, 1:2]).then_inc(ends_summed, 1)
                te.wait_ge(past_made, 1)
                for c in range(per_part + 1):
                    ins = te.matmul(ps_sums[:, 3 * c:3 * c + 3], unit_row[0:blocks - 1, c:c + (P - 1) * per_part + 1:per_part],
                                    steps[0:blocks - 1, :])
                ins.then_inc(units_summed, 1)
                nodes.tensor(te)
                te.wait_ge(tails_counted, 1)
                te.matmul(ps_tails[:, 0:1], earlier[:, :], always[:, :]).then_inc(tails_summed, 1)


def chunks_of(nb):
    return CUTS if nb // GROUP % CUTS == 0 else 1


def layer_norm_relu(e, step, x, out, square, small, nb, to_act, from_act, c):
    width = nb // chunks_of(nb)
    cols = slice(c * width, (c + 1) * width)
    x, out, square = (t[:, cols, :] for t in (x, out, square))
    mean, var, rstd = (t[:, cols] for t in small)
    step(e.tensor_reduce(mean, x, AX.X, ALU.add))
    step(e.tensor_scalar(mean, mean, 1.0 / D, None, ALU.mult))
    step(e.tensor_tensor(out, x, bcast(mean, 2, D), ALU.subtract), to_act)
    e.wait_ge(from_act, 3 * c + 1)
    step(e.tensor_reduce(var, square, AX.X, ALU.add), to_act)
    e.wait_ge(from_act, 3 * c + 2)
    step(e.reciprocal(rstd, rstd))
    step(e.tensor_tensor(out, out, bcast(rstd, 2, D), ALU.mult), to_act)


def layer_norm_act(ac, con, out, final, square, small, nb, to_act, from_act, c):
    width = nb // chunks_of(nb)
    cols = slice(c * width, (c + 1) * width)
    out, final, square = (t[:, cols, 0:D] for t in (out, final, square))
    mean, var, rstd = (t[:, cols] for t in small)
    ac.wait_ge(to_act, 3 * c + 1)
    ac.activation(square, out, ACT.Square).then_inc(from_act, 1)
    ac.wait_ge(to_act, 3 * c + 2)
    ac.activation(rstd, var, ACT.Sqrt, bias=con.eps[0:NB, 0:1], scale=1.0 / D).then_inc(from_act, 1)
    ac.wait_ge(to_act, 3 * c + 3)
    ac.activation(final, out, ACT.Relu).then_inc(from_act, 1)


def node_products_pe(te, con, h, ps_t, ps_o, h_t, weights, width, nb, h_ready, turned, turned_copied,
                     multiplied, products_copied):
    groups = nb // GROUP
    of_chunk = groups // chunks_of(nb)
    for g in range(groups + 1):
        if g < groups:
            if g % of_chunk == 0:
                te.wait_ge(h_ready, 3 * (g // of_chunk) + 3)
            if g >= 2:
                te.wait_ge(turned_copied, g - 1)
            for j in range(GROUP):
                ins = te.transpose(ps_t[g % 2][0:D, j * P:j * P + NB], h[:, g * GROUP + j, 0:D],
                                   con.ident[0:NB, 0:NB])
            ins.then_inc(turned, 1)
        if g >= 1:
            te.wait_ge(turned_copied, g)
            if g >= 3:
                te.wait_ge(products_copied, g - 2)
            for j in range(GROUP):
                ins = te.matmul(ps_o[(g - 1) % 2][0:NB, j * width:(j + 1) * width],
                                h_t[(g - 1) % 2][:, j * P:j * P + NB], weights)
            ins.then_inc(multiplied, 1)


def node_products_copy(e, ps_t, ps_o, h_t, out, width, nb, turned, turned_copied, multiplied,
                       products_copied, normalise):
    groups = nb // GROUP
    of_chunk = groups // chunks_of(nb)
    normalise(0)
    for g in range(groups + 1):
        if g % of_chunk == 0 and g // of_chunk + 1 < chunks_of(nb):
            normalise(g // of_chunk + 1)
        if g < groups:
            e.wait_ge(turned, g + 1)
            if g >= 2:
                e.wait_ge(multiplied, g - 1)
            e.activation(h_t[g % 2][:, :].rearrange("p (j n) -> p j n", n=P)[:, :, 0:NB],
                         ps_t[g % 2][0:D, :].rearrange("p (j n) -> p j n", n=P)[:, :, 0:NB],
                         ACT.Copy).then_inc(turned_copied, 1)
        if g >= 1:
            e.wait_ge(multiplied, g)
            e.activation(out[:, (g - 1) * GROUP:g * GROUP, :],
                         ps_o[(g - 1) % 2][0:NB, 0:GROUP * width].rearrange("p (j w) -> p j w", w=width),
                         ACT.Copy).then_inc(products_copied, 1)


def store_chunks(sp, table, rows_out, nb, products_copied, stored):
    chunks = chunks_of(nb)
    width = nb // chunks
    for c in range(chunks):
        sp.wait_ge(products_copied, width // GROUP * (c + 1))
        cols = slice(c * width, (c + 1) * width)
        sp.dma_start(table.rearrange("(p b) d -> p b d", p=NB)[:, cols, :], rows_out[:, cols, :]
                     ).then_inc(stored, 16)


class FirstNodes:

    def __init__(self, nc, con, ctx, x, attn_l, attn_r, w, table, heads):
        def sb(name, shape, dt=F32):
            return ctx.enter_context(nc.sbuf_tensor(name, shape, dt))

        def ps(name):
            return ctx.enter_context(nc.psum_tensor(name, [P, BANK], F32))
        sem = con.sem
        self.con, self.x, self.attn, self.w, self.table, self.heads = con, x, (attn_l, attn_r), w, table, heads
        self.nb = nb = x.shape[0] // NB
        self.xs, self.sq = sb("n0_x", [NB, nb, D]), sb("n0_sq", [NB, nb, D])
        self.small = [sb(f"n0_small{k}", [NB, nb])[:, :] for k in range(3)]
        self.ws, self.wp = sb("n0_w", [D, heads * D]), sb("n0_wp", [D, 2, heads * D])
        self.wa = sb("n0_wa", [D, 2 * heads])
        self.rows_out = sb("n0_rows", [NB, nb, D + 2 * heads])
        self.h_t = [sb(f"n0_ht{k}", [D, BANK]) for k in range(2)]
        self.ps_t, self.ps_o = [ps(f"n0_pt{k}") for k in range(2)], [ps(f"n0_po{k}") for k in range(2)]
        self.loaded, self.w_loaded, self.chain = sem("n0_loaded"), sem("n0_w_loaded"), sem("n0_chain")
        self.to_act, self.from_act, self.wa_made = sem("n0_to_act"), sem("n0_from_act"), sem("n0_wa_made")
        self.turned, self.turned_copied, self.multiplied, self.products_copied, self.stored = (
            sem("n0_turned"), sem("n0_turned_copied"), sem("n0_multiplied"), sem("n0_products_copied"),
            sem("n0_stored"))

    def load(self, sp):
        sp.dma_start(self.xs[:, :, :], self.x.rearrange("(p b) d -> p b d", p=NB)).then_inc(self.loaded, 16)
        sp.dma_start(self.ws[:, :], self.w).then_inc(self.w_loaded, 16)
        for k, a in enumerate(self.attn):
            sp.dma_start(self.wp[:, k, :], a.rearrange("h d -> (h d)").partition_broadcast(D)
                         ).then_inc(self.w_loaded, 16)

    def store(self, sp):
        store_chunks(sp, self.table, self.rows_out, self.nb, self.products_copied, self.stored)
        sp.wait_ge(self.stored, 16 * chunks_of(self.nb))

    def vector(self, ve):
        step = own_steps(ve, self.chain)
        ve.wait_ge(self.w_loaded, 48)
        step(ve.tensor_tensor(self.wp[:, :, :], self.wp[:, :, :], bcast(self.ws[:, :], 1, 2), ALU.mult))
        step(ve.tensor_reduce(self.wa[:, :], self.wp[:, :, :].rearrange("p k (h d) -> p (k h) d", h=self.heads),
                              AX.X, ALU.add), self.wa_made)
        ve.wait_ge(self.loaded, 16)
        for c in range(chunks_of(self.nb)):
            layer_norm_relu(ve, step, self.xs, self.xs, self.sq, self.small, self.nb, self.to_act,
                            self.from_act, c)

    def scalar(self, ac):
        node_products_copy(ac, self.ps_t, self.ps_o, self.h_t, self.rows_out[:, :, D:], 2 * self.heads, self.nb,
                           self.turned, self.turned_copied, self.multiplied, self.products_copied,
                           lambda c: layer_norm_act(ac, self.con, self.xs, self.rows_out, self.sq, self.small,
                                                    self.nb, self.to_act, self.from_act, c))

    def tensor(self, te):
        te.wait_ge(self.wa_made, 1)
        node_products_pe(te, self.con, self.rows_out, self.ps_t, self.ps_o, self.h_t, self.wa[:, :],
                         2 * self.heads, self.nb, self.from_act, self.turned, self.turned_copied,
                         self.multiplied, self.products_copied)


def extend_weights(sb, name):
    return sb(name + "_wx", [D, ROW]), sb(name + "_as", [D, D]), sb(name + "_ad", [D, D]), sb(name + "_wp", [D, D])


def load_extended(sp, ext, w, a_src, a_dst, loaded):
    wx, a_s, a_d, _ = ext
    sp.dma_start(wx[:, 0:D], w).then_inc(loaded, 16)
    sp.dma_start(a_s[:, :], a_src.partition_broadcast(D)).then_inc(loaded, 16)
    sp.dma_start(a_d[:, :], a_dst.partition_broadcast(D)).then_inc(loaded, 16)


def make_extended(ve, step, ext):
    wx, a_s, a_d, wp = ext
    for k, a in enumerate((a_s, a_d)):
        step(ve.tensor_tensor(wp[:, :], wx[:, 0:D], a[:, :], ALU.mult))
        step(ve.tensor_reduce(wx[:, D + k:D + k + 1], wp[:, :], AX.X, ALU.add))


def middle_nodes(nc, con, x, h0, gamma, beta, w, a_src, a_dst, x_mid, table, n_nodes):
    nb = n_nodes // NB
    with ExitStack() as ctx:
        def sb(name, shape, dt=F32):
            return ctx.enter_context(nc.sbuf_tensor(name, shape, dt))

        def ps(name):
            return ctx.enter_context(nc.psum_tensor(name, [P, BANK], F32))
        sem = con.sem
        xs, hs, sq = sb("n1_x", [NB, nb, D]), sb("n1_h", [NB, nb, D]), sb("n1_sq", [NB, nb, D])
        small = [sb(f"n1_small{k}", [NB, nb])[:, :] for k in range(3)]
        rows_out = sb("n1_rows", [NB, nb, ROW])
        gm, bt = sb("n1_gamma", [NB, D]), sb("n1_beta", [NB, D])
        part, stat, root = sb("n1_part", [NB, D]), sb("n1_stat", [NB, D]), sb("n1_root", [NB, D])
        ext = extend_weights(sb, "n1")
        h_t = [sb(f"n1_ht{k}", [D, BANK]) for k in range(2)]
        ps_t, ps_o = [ps(f"n1_pt{k}") for k in range(2)], [ps(f"n1_po{k}") for k in range(2)]
        ps_stat = ps("n1_stat_ps")
        loaded, w_loaded, chain, w_made = sem("n1_loaded"), sem("n1_w_loaded"), sem("n1_chain"), sem("n1_w_made")
        to_act, from_act = sem("n1_to_act"), sem("n1_from_act")
        centred, squared, var_known, rooted = sem("n1_centred"), sem("n1_squared"), sem("n1_var"), sem("n1_rooted")
        part_made, summed, mid_made = sem("n1_part_made"), sem("n1_summed"), sem("n1_mid_made")
        turned, turned_copied, multiplied, products_copied, stored = (
            sem("n1_turned"), sem("n1_turned_copied"), sem("n1_multiplied"), sem("n1_products_copied"),
            sem("n1_stored"))

        def by_feature(t):
            return t[:, :, :].rearrange("p b d -> p d b")

        with nc.Block() as block:
            @block.sync
            def _(sp):
                sp.dma_start(hs[:, :, :], h0.rearrange("(p b) d -> p b d", p=NB)).then_inc(loaded, 16)
                sp.dma_start(xs[:, :, :], x.rearrange("(p b) d -> p b d", p=NB)).then_inc(loaded, 16)
                sp.dma_start(gm[:, :], gamma.partition_broadcast(NB)).then_inc(loaded, 16)
                sp.dma_start(bt[:, :], beta.partition_broadcast(NB)).then_inc(loaded, 16)
                load_extended(sp, ext, w, a_src, a_dst, w_loaded)
                sp.wait_ge(mid_made, 1)
                sp.dma_start(x_mid.rearrange("(p b) d -> p b d", p=NB), xs[:, :, :]).then_inc(stored, 16)
                store_chunks(sp, table, rows_out, nb, products_copied, stored)
                sp.wait_ge(stored, 16 + 16 * chunks_of(nb))

            @block.vector
            def _(ve):
                step = own_steps(ve, chain)
                ve.wait_ge(w_loaded, 48)
                make_extended(ve, own_steps(ve, w_made), ext)
                ve.wait_ge(loaded, 64)
                step(ve.tensor_reduce(part[:, :], by_feature(hs), AX.X, ALU.add), part_made)
                ve.wait_ge(summed, 1)
                step(ve.tensor_scalar(stat[:, :], ps_stat[0:NB, 0:D], 1.0 / n_nodes, None, ALU.mult))
                step(ve.tensor_tensor(hs[:, :, :], hs[:, :, :], bcast(stat[:, :], 1, nb), ALU.subtract), centred)
                ve.wait_ge(squared, 1)
                step(ve.tensor_reduce(part[:, :], by_feature(sq), AX.X, ALU.add), part_made)
                ve.wait_ge(rooted, 1)
                step(ve.reciprocal(root[:, :], root[:, :]))
                step(ve.tensor_tensor(root[:, :], root[:, :], gm[:, :], ALU.mult))
                step(ve.tensor_tensor(hs[:, :, :], hs[:, :, :], bcast(root[:, :], 1, nb), ALU.mult))
                step(ve.tensor_tensor(hs[:, :, :], hs[:, :, :], bcast(bt[:, :], 1, nb), ALU.add))
                step(ve.scalar_tensor_tensor(xs[:, :, :], hs[:, :, :], 0.0, xs[:, :, :], ALU.max, ALU.add), mid_made)
                for c in range(chunks_of(nb)):
                    layer_norm_relu(ve, step, xs, hs, sq, small, nb, to_act, from_act, c)

            @block.scalar
            def _(ac):
                ac.wait_ge(centred, 1)
                ac.activation(sq[:, :, :], hs[:, :, :], ACT.Square).then_inc(squared, 1)
                ac.wait_ge(summed, 2)
                ac.activation(root[:, :], ps_stat[0:NB, 0:D], ACT.Sqrt, bias=con.eps[0:NB, 0:1],
                              scale=1.0 / n_nodes).then_inc(rooted, 1)
                node_products_copy(ac, ps_t, ps_o, h_t, rows_out, ROW, nb, turned, turned_copied,
                                   multiplied, products_copied,
                                   lambda c: layer_norm_act(ac, con, hs, hs, sq, small, nb, to_act, from_act, c))

            @block.tensor
            def _(te):
                for k in range(2):
                    te.wait_ge(part_made, k + 1)
                    te.matmul(ps_stat[0:NB, 0:D], con.ones[0:NB, 0:NB], part[:, :]).then_inc(summed, 1)
                te.wait_ge(w_made, 4)
                node_products_pe(te, con, hs, ps_t, ps_o, h_t, ext[0][:, :], ROW, nb, from_act, turned,
                                 turned_copied, multiplied, products_copied)


def attention_layer(nc, con, name, units, src, dst, table, out, edge_attr=None, attn_l=None, w_out=None,
                    bias=None, residual=None, next_weights=None):
    unit_ints, unit_floats = units
    first = edge_attr is not None
    heads = 2 if first else 1
    row = D + 2 * heads
    part = D + 1
    vals = 2 * heads
    out_cols = D if (first or residual is not None) else ROW
    OUT_LAG = 3 if residual is None else 2
    PARTS = 3
    SCORE_AT = BANK // 2
    PROJ_AT = P
    MAX_AT = BANK // 2
    with ExitStack() as ctx:
        def sb(tag, shape, dt=F32):
            return ctx.enter_context(nc.sbuf_tensor(f"{name}_{tag}", shape, dt))

        def ps(tag):
            return ctx.enter_context(nc.psum_tensor(f"{name}_{tag}", [P, BANK], F32))

        def sem(tag):
            return con.sem(f"{name}_{tag}")

        def two(make, tag, *args):
            return [make(f"{tag}{k}", *args) for k in range(2)]

        unit_int = two(sb, "unit_int", [1, 4], I32)
        store_int = sb("store_int", [1, 4], I32)
        unit_par = two(sb, "unit_par", [P, 4])
        idx = two(sb, "idx", [P, Q], I32)
        dst_ids = two(sb, "dst_ids", [P, Q], I32)
        rows_in = two(sb, "rows_in", [P, Q, row])
        own = two(sb, "own", [NB, row])
        out_sb = two(sb, "out_sb", [NB, out_cols])
        dst_local = sb("dst_local", [P, Q])
        onehot = two(sb, "onehot", [P, Q, NB])
        onehot_t = sb("onehot_t", [NB, CAP], BF16)
        mask = sb("mask", [P, Q, NB], BF16)
        masked = sb("masked", [P, heads, Q, NB])
        part_max = two(sb, "part_max", [P, heads, NB])
        column_max = sb("column_max", [P, heads, NB])
        max_src = sb("max_src", [NB, heads])
        max_unit = sb("max_unit", [NB, heads])
        max_before = sb("max_before", [NB, heads])
        max_state = sb("max_state", [NB, heads])
        rescale = two(sb, "rescale", [NB, heads])
        node_vals = sb("node_vals", [NB, vals])
        rest = sb("rest", [NB, vals])
        node_split = sb("node_split", [NB, PARTS, vals], BF16)
        edge_vals = sb("edge_vals", [P, Q, vals])
        logits = sb("logits", [P, Q, heads])
        weights = sb("weights", [P, Q, heads])
        weighted = sb("weighted", [P, Q, heads * part])
        acc = sb("acc", [NB, heads * part])
        inverse = sb("inverse", [NB, heads])
        result = sb("result", [NB, heads * D])
        result_t = sb("result_t", [heads * D, NB])
        if first:
            edges = two(sb, "edges", [P, Q, D])
            pairs_t = sb("pairs_t", [P, Q // 2, P])
            edge_scores = sb("edge_scores", [P, Q, heads])
            scores_sum = sb("scores_sum", [P, Q, heads])
            w_cols = sb("w_cols", [P, heads * D])
            al = sb("al", [P, heads * D])
            wl = sb("wl", [P, heads])
            pair_w = sb("pair_w", [P, 2 * heads])
            w_heads = sb("w_heads", [P, D])
        else:
            bias_sb = sb("bias_sb", [NB, D])
            self_row = sb("self_row", [NB, part])
            self_max = sb("self_max", [NB, 1])
            if residual is not None:
                res_sb = two(sb, "res_sb", [NB, D])
            else:
                ext = extend_weights(sb, "ext")

        ps_big = [ps(f"ps_big{g}") for g in range(CHUNKS)]
        ps_edge, ps_acc, ps_out = ps("ps_edge"), ps("ps_acc"), ps("ps_out")

        int_loaded, idx_loaded, meta_loaded, own_loaded, gathered, stored, edges_loaded, res_loaded = (
            two(sem, tag) for tag in ("int_loaded", "idx_loaded", "meta_loaded", "own_loaded",
                                      "gathered", "stored", "edges_loaded", "res_loaded"))
        rows_taken = two(sem, "rows_taken")
        store_int_loaded, w_loaded, w_made, state_set = (
            sem("store_int_loaded"), sem("w_loaded"), sem("w_made"), sem("state_set"))
        chain = sem("chain")
        tails_set, tail_gathered, tail_ready = sem("tails_set"), sem("tail_gathered"), two(sem, "tail_ready")
        passed_sp, passed_gp, passed_te = sem("passed_sp"), sem("passed_gp"), sem("passed_te")
        local_made, onehot_built, turned, onehot_copied, mask_made = (
            sem("local_made"), sem("onehot_built"), sem("turned"), sem("onehot_copied"), sem("mask_made"))
        pairs_turned, pairs_copied, scored, scores_copied, scores_ready = (
            sem("pairs_turned"), sem("pairs_copied"), sem("scored"), sem("scores_copied"), sem("scores_ready"))
        masked_made, columns_maxed, maxima_turned = (
            sem("masked_made"), sem("columns_maxed"), sem("maxima_turned"))
        split_made, expanded, logits_made, weights_made = (
            sem("split_made"), sem("expanded"), sem("logits_made"), sem("weights_made"))
        rows_weighted, aggregated = sem("rows_weighted"), sem("aggregated")
        result_made, result_turned, result_copied, projected, out_made = (
            sem("result_made"), sem("result_turned"), sem("result_copied"), sem("projected"), sem("out_made"))

        def last_pair(eng):
            last = eng.value_load(con.last_unit[0:1, 0:1], min_val=0, max_val=unit_ints.shape[0] - 3)
            return eng.snap(last // 2)

        def unit_pairs(eng):
            return eng.snap(last_pair(eng) + 1)

        assert table.shape[0] // NB > 2

        with nc.Block() as block:
            @block.sync
            def _(sp):
                last = last_pair(sp)
                pairs = sp.snap(last + 1)

                def node0_of(ints):
                    return sp.value_load(ints[0:1, 0:1], min_val=0, max_val=table.shape[0] - NB)

                def load_window(tile, array, edge0, loaded):
                    main, tail = array[bass.ds(edge0, TAIL_AT)], array[bass.ds(edge0 + TAIL_AT, P)]
                    if len(array.shape) == 1:
                        sp.dma_start(tile[:, 0:Q - 1], main.rearrange("(p t) -> p t", p=P)).then_inc(loaded, 16)
                        sp.dma_start(tile[:, Q - 1:Q], tail.rearrange("(p t) -> p t", p=P),
                                     allow_slow_non_contiguous=True).then_inc(loaded, 16)
                    else:
                        sp.dma_start(tile[:, 0:Q - 1, :], main.rearrange("(p t) d -> p t d", p=P)
                                     ).then_inc(loaded, 16)
                        sp.dma_start(tile[:, Q - 1, :], tail).then_inc(loaded, 16)

                def wait_used(sem, value, wait):
                    if wait:
                        wait_apart(sp, sem, value, passed_sp)

                def load_unit(u, h, k, wait):
                    wait_used(gathered[h], 16 * (Q - 1) * k, wait)
                    wait_used(tail_ready[h], k, wait)
                    sp.dma_start(unit_int[h][:, :], unit_ints[bass.ds(u, 1), :]).then_inc(int_loaded[h], 16)
                    wait_apart(sp, int_loaded[h], 16 * k + 16, passed_sp)
                    node0 = node0_of(unit_int[h])
                    edge0 = sp.value_load(unit_int[h][0:1, 1:2], min_val=0, max_val=src.shape[0] - CAP)
                    load_window(idx[h], src, edge0, idx_loaded[h])
                    wait_used(onehot_built, 2 * k + h - 1, wait)
                    load_window(dst_ids[h], dst, edge0, meta_loaded[h])
                    wait_used(rows_weighted, 2 * k + h - 1, wait)
                    sp.dma_start(unit_par[h][:, :], unit_floats[bass.ds(u, 1), :].to_broadcast([P, 4])
                                 ).then_inc(meta_loaded[h], 16)
                    if first:
                        load_window(edges[h], edge_attr, edge0, edges_loaded[h])
                    sp.dma_start(own[h][:, :], table[bass.ds(node0, NB), :]).then_inc(own_loaded[h], 16)

                def load_residual(n, h):
                    if residual is not None:
                        node0 = node0_of(unit_int[h])
                        if not (isinstance(n, int) and n == 0):
                            wait_apart(sp, out_made, n, passed_sp)
                        sp.dma_start(res_sb[h][:, :], residual[bass.ds(node0, NB), :]
                                     ).then_inc(res_loaded[h], 16)

                def store(u, h, k):
                    sp.dma_start(store_int[:, :], unit_ints[bass.ds(u, 1), :]).then_inc(store_int_loaded, 16)
                    wait_apart(sp, store_int_loaded, 16 * u + 16, passed_sp)
                    node0 = node0_of(store_int)
                    wait_apart(sp, stored[1 - h], 16 * k + 32 + 16 * h, passed_sp)
                    wait_apart(sp, out_made, u + OUT_LAG, passed_sp)
                    sp.dma_start(out[bass.ds(node0, NB), :], out_sb[h][:, :]).then_inc(stored[h], 16)

                if first:
                    for half in range(2):
                        sp.dma_start(w_cols[half * D:(half + 1) * D, :], w_out).then_inc(w_loaded, 16)
                        sp.dma_start(w_heads[half * D:(half + 1) * D, :], w_out[:, half * D:(half + 1) * D]
                                     ).then_inc(w_loaded, 16)
                    sp.dma_start(al[:, :], attn_l.rearrange("h d -> (h d)").partition_broadcast(P)
                                 ).then_inc(w_loaded, 16)
                else:
                    sp.dma_start(bias_sb[:, :], bias.partition_broadcast(NB)).then_inc(w_loaded, 16)
                    if next_weights:
                        load_extended(sp, ext, *next_weights, w_loaded)
                for h in range(2):
                    sp.sem_inc(stored[h], 32)
                sp.sem_inc(res_loaded[1], 16)
                load_unit(0, 0, 0, False)
                load_unit(1, 1, 0, False)
                for h in range(2):
                    load_residual(h, h)
                    load_unit(2 + h, h, 1, True)
                with sp.Fori(0, last) as i:
                    for h in range(2):
                        n = sp.snap(2 * i + 2 + h)
                        load_residual(n, h)
                        load_unit(n + 2, h, i + 2, True)
                        store(sp.snap(2 * i + h), h, i)
                for h in range(2):
                    store(sp.snap(2 * last + h), h, last)
                for h in range(2):
                    wait_apart(sp, idx_loaded[h], 32 * pairs + 32, passed_sp)
                    wait_apart(sp, meta_loaded[h], 48 * pairs + 48, passed_sp)
                    wait_apart(sp, own_loaded[h], 16 * pairs + 16, passed_sp)
                    if first:
                        wait_apart(sp, edges_loaded[h], 32 * pairs + 32, passed_sp)
                    wait_apart(sp, stored[h], 16 * pairs + 32, passed_sp)

            @block.gpsimd
            def _(gp):
                pairs = unit_pairs(gp)

                def gather(h, t, done):
                    gp.indirect_dma_start(rows_in[h][:, t, :], None, table[:, :],
                                          bass.IndirectOffsetOnAxis(ap=idx[h][:, t:t + 1], axis=0)
                                          ).then_inc(done, 16)

                for h in range(2):
                    gp.memset(rows_in[h][:, Q - 1, :], 0.0).then_inc(tails_set, 1)
                gp.wait_ge(tails_set, 2)
                with gp.Fori(0, pairs) as i:
                    for h in range(2):
                        gp.wait_ge(rows_taken[h], i + 1)
                        wait_apart(gp, idx_loaded[h], 32 * i + 32, passed_gp)
                        has_tail = gp.value_load(unit_int[h][0:1, 2:3], min_val=0, max_val=1)
                        tails = gp.value_load(unit_int[h][0:1, 3:4], min_val=1, max_val=unit_ints.shape[0])
                        with gp.If(has_tail > 0):
                            gather(h, Q - 1, tail_gathered)
                        for t in range(Q - 1):
                            gather(h, t, gathered[h])
                        with gp.If(has_tail > 0):
                            wait_apart(gp, tail_gathered, 16 * tails, passed_gp)
                        gp.sem_inc(tail_ready[h], 1)

            @block.vector
            def _(ve):
                pairs = unit_pairs(ve)
                STEPS = 24 if first else 25

                ve.wait_ge(w_loaded, 5 * 16 if first else 4 * 16 if next_weights else 16)
                if first:
                    step = own_steps(ve, w_made)
                    step(ve.tensor_tensor(al[:, :], al[:, :], w_cols[:, :], ALU.mult))
                    step(ve.tensor_reduce(wl[:, :], al[:, :].rearrange("p (h d) -> p h d", h=heads), AX.X,
                                          ALU.add))
                    step(ve.memset(pair_w[:, :], 0.0))
                    step(ve.tensor_copy(pair_w[0:D, 0:heads], wl[0:D, :]))
                    step(ve.tensor_copy(pair_w[D:P, heads:2 * heads], wl[D:P, :]))
                elif next_weights:
                    make_extended(ve, own_steps(ve, w_made), ext)
                step = own_steps(ve, state_set)
                step(ve.memset(acc[:, :], 0.0))
                step(ve.memset(rescale[1][:, :], 0.0))
                step(ve.memset(max_state[:, :], 0.0))
                step(ve.memset(ps_acc[0:NB, 0:heads * part], 0.0))
                if residual is not None:
                    step(ve.memset(res_sb[1][:, :], 0.0))
                step(ve.memset(ps_out[:, :], 0.0))
                ve.sem_inc(result_turned, 1)

                def localize(k, h):
                    ve.wait_ge(meta_loaded[h], 48 * k + 48)
                    ve.tensor_scalar(dst_local[:, :], dst_ids[h][:, :], unit_par[h][:, 0:1], None,
                                     ALU.subtract).then_inc(local_made, 1)

                def build_onehot(n, h):
                    ve.wait_ge(local_made, n + 1)
                    ve.tensor_tensor(onehot[h][:, :, :], bcast(con.iota_nodes[:, :], 1, Q),
                                     bcast(dst_local[:, :], 2, NB), ALU.is_equal).then_inc(onehot_built, 1)

                def finish(i, h, n, step):
                    ve.wait_ge(weights_made, 2 * n + 2)
                    for hd in range(heads):
                        span = slice(hd * part, (hd + 1) * part)
                        step(ve.scalar_tensor_tensor(acc[:, span], acc[:, span], rescale[1 - h][:, hd:hd + 1],
                                                     ps_acc[0:NB, span], ALU.mult, ALU.add))
                    step(ve.tensor_scalar(inverse[:, :], acc[:, D::part], 1e-16, None, ALU.add))
                    step(ve.reciprocal(inverse[:, :], inverse[:, :]))
                    if first:
                        step(ve.tensor_scalar(result[:, 0:D], acc[:, 0:D], inverse[:, 0:1], None, ALU.mult))
                        ve.tensor_scalar(result[:, D:2 * D], acc[:, part:part + D], inverse[:, 1:2], None,
                                         ALU.mult).then_inc(result_made, 1)
                        return
                    ve.scalar_tensor_tensor(result[:, :], acc[:, 0:D], inverse[:, 0:1], bias_sb[:, :],
                                            ALU.mult, ALU.add).then_inc(result_made, 1)
                    if residual is not None:
                        ve.wait_ge(result_made, n + 1)
                        ve.wait_ge(res_loaded[1 - h], 16 * i + 16)
                        ve.wait_ge(stored[1 - h], 16 * i + 16 + 16 * h)
                        ve.tensor_tensor(out_sb[1 - h][:, :], result[:, :], res_sb[1 - h][:, :], ALU.add
                                         ).then_inc(out_made, 1)

                def begin(h, step):
                    carries, begins, low = (unit_par[h][0:NB, k:k + 1] for k in (1, 2, 3))
                    step(ve.tensor_copy(node_vals[:, 0:heads], own[h][:, D + heads:row]))
                    if first:
                        step(ve.tensor_scalar(max_before[:, :], max_state[:, :], carries, low, ALU.mult, ALU.add))
                        return
                    step(ve.tensor_tensor(self_max[:, :], own[h][:, D:D + 1], own[h][:, D + 1:D + 2], ALU.add))
                    step(ve.scalar_tensor_tensor(self_max[:, :], self_max[:, :], SLOPE, self_max[:, :],
                                                 ALU.mult, ALU.max))
                    step(ve.tensor_scalar(self_max[:, :], self_max[:, :], begins, None, ALU.mult))
                    step(ve.scalar_tensor_tensor(max_before[:, :], max_state[:, :], carries, self_max[:, :],
                                                 ALU.mult, ALU.add))
                    ve.tensor_scalar(self_row[:, 0:D], own[h][:, 0:D], begins, None, ALU.mult)
                    step(ve.tensor_copy(self_row[:, D:part], begins))

                def begin_sums(n, h, step):
                    ve.wait_ge(result_made, n + 1)
                    step(ve.scalar_tensor_tensor(acc[:, :], acc[:, :], unit_par[h][0:NB, 1:2], self_row[:, :],
                                                 ALU.mult, ALU.add))

                def weigh(i, h, n, k_next, step):
                    ve.wait_ge(gathered[h], 16 * (Q - 1) * i + 16 * (Q - 1))
                    ve.wait_ge(tail_ready[h], i + 1)
                    ve.wait_ge(own_loaded[h], 16 * i + 16)
                    if first:
                        ve.wait_ge(scores_copied, n + 1)
                        ve.wait_ge(edges_loaded[h], 32 * i + 32)
                        ve.tensor_tensor(scores_sum[:, :, :], edge_scores[:, :, :], rows_in[h][:, :, D:D + heads],
                                         ALU.add).then_inc(scores_ready, 1)
                        ve.tensor_tensor(edges[h][:, :, :], edges[h][:, :, :], rows_in[h][:, :, 0:D], ALU.add
                                         ).then_inc(rows_taken[h], 1)
                    begin(h, step)
                    localize(k_next, 1 - h)
                    if not first:
                        ve.wait_ge(aggregated, n + 1)
                        build_onehot(n + 1, 1 - h)
                    for hd in range(heads):
                        for k, cols in enumerate((slice(0, EARLY), slice(EARLY, Q))):
                            ve.wait_ge(masked_made, 2 * (heads * n + hd) + k + 1)
                            step(ve.tensor_reduce(part_max[k][:, hd, :], masked[:, hd, cols, :]
                                                  .rearrange("p t n -> p n t"), AX.X, ALU.max))
                        ve.tensor_tensor(column_max[:, hd, :], part_max[0][:, hd, :], part_max[1][:, hd, :], ALU.max
                                         ).then_inc(columns_maxed, 1)
                        if first and hd == 0:
                            ve.wait_ge(aggregated, n + 1)
                            build_onehot(n + 1, 1 - h)
                    finish(i, h, n, step)
                    if not first:
                        begin_sums(n, h, step)
                    ve.wait_ge(maxima_turned, n + 1)
                    step(ve.tensor_reduce(max_src[:, :], ps_edge[0:NB, MAX_AT:MAX_AT + heads * P]
                                          .rearrange("p (h e) -> p h e", h=heads), AX.X, ALU.max))
                    step(ve.tensor_tensor(max_unit[:, :], node_vals[:, 0:heads], max_src[:, :], ALU.add))
                    step(ve.scalar_tensor_tensor(max_unit[:, :], max_unit[:, :], SLOPE, max_unit[:, :],
                                                 ALU.mult, ALU.max))
                    step(ve.tensor_tensor(node_vals[:, heads:vals], max_before[:, :], max_unit[:, :], ALU.max))
                    step(ve.tensor_copy(node_split[:, 0, :], node_vals[:, :]))
                    step(ve.tensor_tensor(rest[:, :], node_vals[:, :], node_split[:, 0, :], ALU.subtract))
                    step(ve.tensor_copy(node_split[:, 1, :], rest[:, :]))
                    ve.tensor_tensor(node_split[:, 2, :], rest[:, :], node_split[:, 1, :], ALU.subtract
                                     ).then_inc(split_made, 1)
                    step(ve.tensor_tensor(rescale[h][:, :], max_before[:, :], node_vals[:, heads:vals],
                                          ALU.subtract))
                    step(ve.tensor_copy(max_state[:, :], node_vals[:, heads:vals]))
                    ve.wait_ge(expanded, n + 1)
                    step(ve.tensor_reduce(edge_vals[:, :, :], ps_edge[:, 0:Q * PARTS * vals]
                                          .rearrange("p (t s k) -> p t k s", s=PARTS, k=vals), AX.X, ALU.add))
                    scores = scores_sum[:, :, :] if first else rows_in[h][:, :, D:D + 1]
                    step(ve.tensor_tensor(logits[:, :, :], scores, edge_vals[:, :, 0:heads], ALU.add))
                    step(ve.scalar_tensor_tensor(logits[:, :, :], logits[:, :, :], SLOPE, logits[:, :, :],
                                                 ALU.mult, ALU.max))
                    step(ve.tensor_tensor(logits[:, :, :], logits[:, :, :], edge_vals[:, :, heads:vals],
                                          ALU.subtract))
                    ve.tensor_scalar(logits[:, :, :], logits[:, :, :], 0.0, None, ALU.min).then_inc(logits_made, 1)
                    ve.wait_ge(weights_made, 2 * n + 3)
                    rows = edges[h] if first else rows_in[h]
                    for hd in range(heads):
                        ins = ve.tensor_tensor(weighted[:, :, hd * part:hd * part + D], rows[:, :, 0:D],
                                               bcast(weights[:, :, hd], 2, D), ALU.mult)
                    if not first:
                        ins.then_inc(rows_taken[h], 1)
                    ve.tensor_copy(weighted[:, :, D::part], weights[:, :, :]).then_inc(rows_weighted, 1)

                for h in range(2):
                    ve.sem_inc(rows_taken[h], 1)
                localize(0, 0)
                build_onehot(0, 0)
                with ve.Fori(0, pairs) as i:
                    for h in range(2):
                        n = ve.snap(2 * i + h)
                        step = own_steps(ve, chain, ve.snap(n * STEPS))
                        weigh(i, h, n, i + h, step)
                        assert step.taken() == STEPS, step.taken()
                n = ve.snap(2 * pairs)
                ve.wait_ge(aggregated, n + 1)
                finish(pairs, 0, n, own_steps(ve, chain, ve.snap(n * STEPS)))

            @block.scalar
            def _(ac):
                pairs = unit_pairs(ac)

                def copy_pairs(n):
                    ac.wait_ge(pairs_turned, n + 1)
                    for j0 in range(0, Q // 2, GROUP):
                        j1 = min(j0 + GROUP, Q // 2)
                        ins = ac.activation(
                            pairs_t[:, j0:j1, :],
                            ps_big[j0 // GROUP][:, 0:(j1 - j0) * P].rearrange("p (j e) -> p j e", e=P),
                            ACT.Copy)
                    ins.then_inc(pairs_copied, 1)

                def copy_scores(n):
                    ac.wait_ge(scored, n + 1)
                    ac.activation(edge_scores[:, :, :], ps_out[:, SCORE_AT:SCORE_AT + Q * heads]
                                  .rearrange("p (t k) -> p t k", k=heads), ACT.Copy
                                  ).then_inc(scores_copied, 1)

                def make_mask(n, h):
                    ac.wait_ge(onehot_built, n + 1)
                    ac.activation(mask[:, :, :], onehot[h][:, :, :], ACT.Copy, bias=-BIG, scale=BIG
                                  ).then_inc(mask_made, 1)

                def copy_result(n):
                    if residual is None:
                        ac.wait_ge(result_turned, n + 1)
                        ac.activation(result_t[:, :], ps_out[0:heads * D, 0:NB], ACT.Copy if first else ACT.Relu
                                      ).then_inc(result_copied, 1)

                def copy_out(i, h, n):
                    if residual is None:
                        ac.wait_ge(projected, n + 1)
                        ac.wait_ge(stored[h], 16 * i + 16)
                        ac.activation(out_sb[h][:, :], ps_out[0:NB, PROJ_AT:PROJ_AT + out_cols], ACT.Copy,
                                      scale=1.0 / heads).then_inc(out_made, 1)

                ac.sem_inc(weights_made, 1)
                ac.wait_ge(state_set, 2)
                ac.activation(rescale[1][:, :], rescale[1][:, :], ACT.Exp).then_inc(weights_made, 1)
                if first:
                    copy_pairs(0)
                    copy_scores(0)
                make_mask(0, 0)
                with ac.Fori(0, pairs) as i:
                    for h in range(2):
                        n = ac.snap(2 * i + h)
                        ac.wait_ge(mask_made, n + 1)
                        if first:
                            ac.wait_ge(scores_ready, n + 1)
                        else:
                            ac.wait_ge(gathered[h], 16 * (Q - 1) * i + 16 * (Q - 1))
                            ac.wait_ge(tail_ready[h], i + 1)
                        for hd in range(heads):
                            for t in range(Q):
                                score = scores_sum[:, t, hd:hd + 1] if first else rows_in[h][:, t, D:D + 1]
                                ins = ac.activation(masked[:, hd, t, :], mask[:, t, :], ACT.Identity, bias=score)
                                if t in (EARLY - 1, Q - 1):
                                    ins.then_inc(masked_made, 1)
                        ac.wait_ge(turned, n + 1)
                        for g in range(CHUNKS):
                            cols = len(chunk_cols(g)) * P
                            ins = ac.activation(onehot_t[:, g * BANK:g * BANK + cols], ps_big[g][0:NB, 0:cols],
                                                ACT.Copy)
                        ins.then_inc(onehot_copied, 1)
                        copy_result(n)
                        if first:
                            copy_pairs(n + 1)
                        if not first:
                            ac.wait_ge(masked_made, 2 * n + 2)
                            make_mask(n + 1, 1 - h)
                        ac.wait_ge(logits_made, n + 1)
                        ac.activation(weights[:, :, :], logits[:, :, :], ACT.Exp).then_inc(weights_made, 1)
                        ac.activation(rescale[h][:, :], rescale[h][:, :], ACT.Exp).then_inc(weights_made, 1)
                        if first:
                            make_mask(n + 1, 1 - h)
                            ac.wait_ge(scored, n + 2)
                        copy_out(i, h, n)
                        if first:
                            copy_scores(n + 1)
                for h in range(2):
                    n = ac.snap(2 * pairs + h)
                    copy_result(n)
                    copy_out(pairs, h, n)

            @block.tensor
            def _(te):
                pairs = unit_pairs(te)

                def turn_pairs(n, k, h):
                    te.wait_ge(edges_loaded[h], 32 * k + 32)
                    for j in range(Q // 2):
                        ins = te.transpose(ps_big[j // GROUP][:, j % GROUP * P:(j % GROUP + 1) * P],
                                           edges[h][:, 2 * j:2 * j + 2, :].rearrange("p t d -> p (t d)"),
                                           con.ident[:, :])
                    ins.then_inc(pairs_turned, 1)

                def score_pairs(n):
                    te.wait_ge(pairs_copied, n + 1)
                    for j in range(Q // 2):
                        at = SCORE_AT + 2 * heads * j
                        ins = te.matmul(ps_out[:, at:at + 2 * heads], pairs_t[:, j, :], pair_w[:, :])
                    ins.then_inc(scored, 1)

                def turn_onehot(n, h):
                    te.wait_ge(onehot_built, n + 1)
                    for t in range(Q):
                        ins = te.transpose(ps_big[t // GROUP][0:NB, t % GROUP * P:(t % GROUP + 1) * P],
                                           onehot[h][:, t, :], con.ident[:, :])
                    ins.then_inc(turned, 1)

                def project(n):
                    if residual is None:
                        te.wait_ge(result_copied, n + 1)
                        te.matmul(ps_out[0:NB, PROJ_AT:PROJ_AT + out_cols], result_t[:, :],
                                  w_heads[:, :] if first else ext[0][:, :]).then_inc(projected, 1)

                def turn_result(n):
                    if residual is None:
                        te.wait_ge(out_made, n + 1)
                        wait_apart(te, result_made, n + 1, passed_te)
                        te.transpose(ps_out[0:heads * D, 0:NB], result[:, :], con.ident[0:NB, 0:NB]
                                     ).then_inc(result_turned, 1)

                te.sem_inc(aggregated, 1)
                te.wait_ge(result_turned, 1)
                if first:
                    te.wait_ge(w_made, 5)
                    turn_pairs(0, 0, 0)
                    score_pairs(0)
                elif next_weights:
                    te.wait_ge(w_made, 4)
                turn_onehot(0, 0)
                with te.Fori(0, pairs) as i:
                    for h in range(2):
                        n = te.snap(2 * i + h)
                        te.wait_ge(columns_maxed, heads * n + heads)
                        for hd in range(heads):
                            ins = te.transpose(ps_edge[0:NB, MAX_AT + hd * P:MAX_AT + (hd + 1) * P],
                                               column_max[:, hd, :], con.ident[:, :])
                        ins.then_inc(maxima_turned, 1)
                        te.wait_ge(onehot_copied, n + 1)
                        if first:
                            turn_pairs(n + 1, i + h, 1 - h)
                        te.wait_ge(split_made, n + 1)
                        for t in range(Q):
                            ins = te.matmul(ps_edge[:, PARTS * vals * t:PARTS * vals * (t + 1)],
                                            onehot_t[:, t * P:(t + 1) * P],
                                            node_split[:, :, :].rearrange("p s k -> p (s k)"))
                        ins.then_inc(expanded, 1)
                        project(n)
                        if first:
                            score_pairs(n + 1)
                        else:
                            turn_onehot(n + 1, 1 - h)
                        if first:
                            te.wait_ge(scores_copied, n + 2)
                        turn_result(n)
                        te.wait_ge(rows_weighted, n + 1)
                        for t in range(Q):
                            ins = te.matmul(ps_acc[0:NB, 0:heads * part], onehot[h][:, t, :], weighted[:, t, :],
                                            start=t == 0, stop=t == Q - 1)
                        ins.then_inc(aggregated, 1)
                        if first:
                            turn_onehot(n + 1, 1 - h)
                n = te.snap(2 * pairs)
                project(n)
                turn_result(n)
                project(te.snap(n + 1))


def graph_network(nc, n_nodes, n_edges, x, src, dst, edge_attr, w0, attn_l, attn_r, gamma, beta, w1, a1s,
                  a1d, b1, w2, a2s, a2d, b2, w3, a3s, a3d, b3, out):
    blocks = n_nodes // NB
    rounds = -(-n_edges // CAP)
    grid = -(-(blocks * rounds + 2) // P) * P

    def dram(name, shape, dt=F32):
        return nc.dram_tensor(name, shape, dt).ap()
    unit_ints, unit_floats = dram("unit_ints", (grid, 4), I32), dram("unit_floats", (grid, 4))
    h_in = dram("h_in", (n_nodes, D + 4))
    h_heads, x_mid = dram("h_heads", (n_nodes, D)), dram("x_mid", (n_nodes, D))
    tables = [dram(f"table{k}", (n_nodes, ROW)) for k in range(3)]
    units = unit_ints, unit_floats
    with ExitStack() as ctx:
        con = Constants(nc, ctx)
        list_units(nc, con, dst, unit_ints, unit_floats, n_nodes, n_edges,
                   lambda phase: FirstNodes(nc, con, phase, x, attn_l, attn_r, w0, h_in, 2))
        con.end_phase()
        attention_layer(nc, con, "heads", units, src, dst, h_in, h_heads,
                        edge_attr=edge_attr, attn_l=attn_l, w_out=w0)
        con.end_phase()
        middle_nodes(nc, con, x, h_heads, gamma, beta, w1, a1s, a1d, x_mid, tables[0], n_nodes)
        plain = [(b1, (w2, a2s, a2d)), (b2, (w3, a3s, a3d)), (b3, None)]
        for k, (bias, following) in enumerate(plain):
            con.end_phase()
            attention_layer(nc, con, f"plain{k}", units, src, dst, tables[k],
                            tables[k + 1] if following else out, bias=bias, next_weights=following,
                            residual=None if following else x_mid)


NAMES = ["x", "src", "dst", "edge_attr_64", "L0_gnn_W", "L0_gnn_attn_l", "L0_gnn_attn_r", "L0_gnn_bn_gamma",
         "L0_gnn_bn_beta", "L1_gnn_W1", "L1_gnn_a1s", "L1_gnn_a1d", "L1_gnn_b1", "L1_gnn_W2", "L1_gnn_a2s",
         "L1_gnn_a2d", "L1_gnn_b2", "L1_gnn_W3", "L1_gnn_a3s", "L1_gnn_a3d", "L1_gnn_b3"]


def kernel(**inputs):
    import numpy as np
    import concourse.bacc as bacc
    from concourse.bass_utils import run_bass_kernel_spmd

    arrays = {name: np.ascontiguousarray(inputs[name]) for name in NAMES}
    n_nodes, n_edges = arrays["x"].shape[0], arrays["src"].shape[0]
    for name, fill in (("src", 0), ("dst", 2 * n_nodes), ("edge_attr_64", 0)):
        a = arrays[name]
        arrays[name] = np.concatenate([a, np.full((CAP,) + a.shape[1:], fill, a.dtype)])
    nc = bacc.Bacc("TRN2", target_bir_lowering=False, num_devices=1)
    args = [nc.dram_tensor("in_" + name, arrays[name].shape, mybir.dt.from_np(arrays[name].dtype),
                           kind="ExternalInput").ap() for name in NAMES]
    out = nc.dram_tensor("out", (n_nodes, D), F32, kind="ExternalOutput").ap()
    graph_network(nc, n_nodes, n_edges, *args, out)
    r = run_bass_kernel_spmd(nc, [{"in_" + name: arrays[name] for name in NAMES}], core_ids=[0])
    return r.results[0]["out"]
```
